# Optimizing a Trainium2 kernel written in Bass

```python
import numpy as np
import jax
import jax.numpy as jnp

def _softmax(x, axis=-1):
    return jax.nn.softmax(x, axis=axis)

def _gelu(x):
    return jax.nn.gelu(x, approximate=True)

def _silu(x):
    return jax.nn.silu(x)

def _sigmoid(x):
    return jax.nn.sigmoid(x)

def _layernorm(x, axis=-1, eps=1e-05):
    m = jnp.mean(x, axis=axis, keepdims=True)
    v = jnp.var(x, axis=axis, keepdims=True)
    return (x - m) / jnp.sqrt(v + eps)

def _scatter_add(tgt, idx, src, axis=0):
    return tgt.at[idx].add(src)

def _segment_sum(src, seg, n):
    return jax.ops.segment_sum(src, seg, n)
kernel_name = 'mk_gnn_resnorm_d2_gnn_r32_e4babc'

def setup_inputs(seed: int=0):
    np.random.seed(seed)
    _w = jnp.asarray

    def _rec_inputs():
        import jax
        import jax.numpy as jnp
        _gk = jax.random.key(seed)
        x = -0.0003713 + 1 * jax.random.normal(jax.random.fold_in(_gk, 1), (3125, 128), jnp.float32)
        _s = jax.random.randint(jax.random.fold_in(_gk, 2), (25000,), 0, 3125, jnp.int32)
        _d = jax.random.randint(jax.random.fold_in(_gk, 3), (25000,), 0, 3125, jnp.int32)
        _loop = jnp.arange(3125, dtype=jnp.int32)
        src = jnp.concatenate([_s, _d, _loop])
        dst = jnp.concatenate([_d, _s, _loop])
        _o = jnp.argsort(dst, stable=True)
        src = src[_o]
        dst = dst[_o]
        edge_type_64 = jax.random.randint(jax.random.fold_in(_gk, 12), (53125,), 0, 64, jnp.int32)
        return (x, src, dst, edge_type_64)
    x, src, dst, edge_type_64 = _rec_inputs()

    def _L0_gnn_setup():
        import jax, jax.numpy as jnp
        import numpy as np
        N_NODES = 3125
        N_EDGES = 18750
        HIDDEN = 128
        NUM_REL = 64
        key = jax.random.key(seed)
        ks = jax.random.split(key, 8)
        node_states = jax.random.normal(ks[0], (N_NODES, HIDDEN), dtype=jnp.float32)
        edge_index = jax.random.randint(ks[1], (2, N_EDGES), 0, N_NODES, dtype=jnp.int64)
        edge_type_ids = jax.random.randint(ks[2], (N_EDGES,), 0, NUM_REL, dtype=jnp.int64)
        s = 1.0 / np.sqrt(HIDDEN)
        W_self = jax.random.uniform(ks[3], (HIDDEN, HIDDEN), jnp.float32, -s, s)
        b_self = jax.random.uniform(ks[4], (HIDDEN,), jnp.float32, -s, s)
        W_msg = jax.random.uniform(ks[5], (HIDDEN, HIDDEN), jnp.float32, -s, s)
        b_msg = jax.random.uniform(ks[6], (HIDDEN,), jnp.float32, -s, s)
        rel_emb = jax.random.normal(ks[7], (NUM_REL, HIDDEN), dtype=jnp.float32)
        return {'node_states': node_states, 'edge_index': edge_index, 'edge_type_ids': edge_type_ids, 'W_self': W_self, 'b_self': b_self, 'W_msg': W_msg, 'b_msg': b_msg, 'rel_emb': rel_emb}
    _L0_gnn_all = _L0_gnn_setup()
    _L0_gnn_in = {k: v for k, v in _L0_gnn_all.items() if k in ('W_self', 'b_self', 'W_msg', 'b_msg', 'rel_emb')}
    del _L0_gnn_all

    def _L1_gnn_setup():
        import jax, jax.numpy as jnp
        import numpy as np
        N_NODES = 3125
        N_EDGES = 25000
        D = 128

        def segment_mean(vals, seg_ids, num_segments):
            summed = jax.ops.segment_sum(vals, seg_ids, num_segments=num_segments)
            deg = jax.ops.segment_sum(jnp.ones((vals.shape[0],), vals.dtype), seg_ids, num_segments=num_segments)
            return summed / jnp.maximum(deg, 1.0)[:, None]

        def sage_conv(x, src, dst, W_l, W_r, b, num_nodes):
            agg = segment_mean(x[src], dst, num_nodes)
            return agg @ W_l.T + b + x @ W_r.T

        def swish(h):
            return h * jax.nn.sigmoid(h)
        key = jax.random.key(seed)
        ks = jax.random.split(key, 8)
        s = 1.0 / np.sqrt(D)
        return {'x': jax.random.normal(ks[0], (N_NODES, D), jnp.float32), 'edge_index': jax.random.randint(ks[1], (2, N_EDGES), 0, N_NODES, jnp.int64), 'W1_l': jax.random.uniform(ks[2], (D, D), jnp.float32, -s, s), 'W1_r': jax.random.uniform(ks[3], (D, D), jnp.float32, -s, s), 'b1': jnp.zeros((D,), jnp.float32), 'W2_l': jax.random.uniform(ks[4], (D, D), jnp.float32, -s, s), 'W2_r': jax.random.uniform(ks[5], (D, D), jnp.float32, -s, s), 'b2': jnp.zeros((D,), jnp.float32)}
    _L1_gnn_all = _L1_gnn_setup()
    _L1_gnn_in = {k: v for k, v in _L1_gnn_all.items() if k in ('W1_l', 'W1_r', 'b1', 'W2_l', 'W2_r', 'b2')}
    del _L1_gnn_all
    return {'x': x, 'src': src, 'dst': dst, 'edge_type_64': edge_type_64, 'L0_gnn_W_self': _L0_gnn_in['W_self'], 'L0_gnn_b_self': _L0_gnn_in['b_self'], 'L0_gnn_W_msg': _L0_gnn_in['W_msg'], 'L0_gnn_b_msg': _L0_gnn_in['b_msg'], 'L0_gnn_rel_emb': _L0_gnn_in['rel_emb'], 'L1_gnn_W1_l': _L1_gnn_in['W1_l'], 'L1_gnn_W1_r': _L1_gnn_in['W1_r'], 'L1_gnn_b1': _L1_gnn_in['b1'], 'L1_gnn_W2_l': _L1_gnn_in['W2_l'], 'L1_gnn_W2_r': _L1_gnn_in['W2_r'], 'L1_gnn_b2': _L1_gnn_in['b2']}

def reference(x, src, dst, edge_type_64, L0_gnn_W_self, L0_gnn_b_self, L0_gnn_W_msg, L0_gnn_b_msg, L0_gnn_rel_emb, L1_gnn_W1_l, L1_gnn_W1_r, L1_gnn_b1, L1_gnn_W2_l, L1_gnn_W2_r, L1_gnn_b2):
    import jax
    import jax.numpy as jnp

    def _L0_gnn_ref(node_states, edge_index, edge_type_ids, W_self, b_self, W_msg, b_msg, rel_emb):
        import jax, jax.numpy as jnp
        import numpy as np
        N_NODES = 3125
        N_EDGES = 18750
        HIDDEN = 128
        NUM_REL = 64
        src = edge_index[0]
        dst = edge_index[1]
        n_nodes = node_states.shape[0]
        rel_ids = jnp.clip(edge_type_ids, 0, rel_emb.shape[0] - 1)
        rel_vec = rel_emb[rel_ids]
        msg = (node_states[src] + rel_vec) @ W_msg.T + b_msg
        agg = jax.ops.segment_sum(msg, dst, num_segments=n_nodes)
        deg = jax.ops.segment_sum(jnp.ones((dst.shape[0],), node_states.dtype), dst, num_segments=n_nodes)
        agg = agg / jnp.maximum(deg, 1.0)[:, None]
        return node_states @ W_self.T + b_self + agg

    def _L1_gnn_ref(x, edge_index, W1_l, W1_r, b1, W2_l, W2_r, b2):
        import jax, jax.numpy as jnp
        import numpy as np
        N_NODES = 3125
        N_EDGES = 25000
        D = 128

        def segment_mean(vals, seg_ids, num_segments):
            summed = jax.ops.segment_sum(vals, seg_ids, num_segments=num_segments)
            deg = jax.ops.segment_sum(jnp.ones((vals.shape[0],), vals.dtype), seg_ids, num_segments=num_segments)
            return summed / jnp.maximum(deg, 1.0)[:, None]

        def sage_conv(x, src, dst, W_l, W_r, b, num_nodes):
            agg = segment_mean(x[src], dst, num_nodes)
            return agg @ W_l.T + b + x @ W_r.T

        def swish(h):
            return h * jax.nn.sigmoid(h)
        src, dst = (edge_index[0], edge_index[1])
        n = x.shape[0]
        h = sage_conv(x, src, dst, W1_l, W1_r, b1, n)
        h = swish(h)
        out = sage_conv(h, src, dst, W2_l, W2_r, b2, n)
        return out
    edge_index = jnp.stack([src, dst])
    x = _layernorm(x + _L0_gnn_ref(x, edge_index, edge_type_64, L0_gnn_W_self, L0_gnn_b_self, L0_gnn_W_msg, L0_gnn_b_msg, L0_gnn_rel_emb), axis=-1)
    x = _layernorm(x + _L1_gnn_ref(x, edge_index, L1_gnn_W1_l, L1_gnn_W1_r, L1_gnn_b1, L1_gnn_W2_l, L1_gnn_W2_r, L1_gnn_b2), axis=-1)
    return x

_drawn_inputs = setup_inputs


def setup_inputs(seed=0):
    import zlib

    import numpy as np

    out = dict(_drawn_inputs(seed))
    spreads = {'L1_gnn_b1': (0.0, 0.1), 'L1_gnn_b2': (0.0, 0.1)}
    factors = {}
    for name, (base, spread) in spreads.items():
        noise = np.random.default_rng([zlib.crc32(name.encode()), seed]).standard_normal(out[name].shape)
        drawn = base * np.exp(spread * noise) if base else spread * noise
        out[name] = jnp.asarray(drawn.astype(out[name].dtype))
    for name, factor in factors.items():
        out[name] = (out[name] * factor).astype(out[name].dtype)
    return out
```

```python
from contextlib import ExitStack

import numpy as np

import concourse.bass as bass
from concourse import mybir

ALU = mybir.AluOpType
ACT = mybir.ActivationFunctionType
AX = mybir.AxisListType
F32 = mybir.dt.float32
F16 = mybir.dt.float16
I32 = mybir.dt.int32
U32 = mybir.dt.uint32
DVE = mybir.EngineType.DVE

P = 128
N = 3125
D = 128
E = 53125
RELATIONS = 64
TILES = 416
FULL_TILES = E // P
GROUP = 2
GROUPS = TILES // GROUP
DEPTH = 2
WINDOW = 24
BLOCKS = (N + P - 1) // P
ROWS = BLOCKS + 1
HALF = ROWS // 2
COMBINED = BLOCKS * WINDOW
WIDTH = 3152
CHUNK = 512
CHUNKS = (N + CHUNK - 1) // CHUNK
LAST = N - CHUNK * (CHUNKS - 1)
SUB = CHUNK // P
SPLIT = 2048.0
EARLY = 5
PERIOD = 34
LEAD = 40
PER_STEP = 2
STEPS = (ROWS - 2) // PER_STEP
EARLY_DONE = STEPS * DEPTH
MOST_EDGES = 2048.0
MOST_VALUE = 60000.0
PEAKS = 3 + 2 * CHUNKS
EPS = 1e-5
NO_NODE = 4096
WEIGHTS = ("w_msg", "w_self", "w1_l", "w1_r", "w2_l", "w2_r")
assert LEAD + PERIOD * (EARLY - 1) + EARLY_DONE < GROUPS - DEPTH and ROWS % 2 == 0
assert WIDTH >= N - 1 + WINDOW and HALF * WINDOW <= 512 and LAST <= P and CHUNKS == 7


def gnn_program(nc, x, src_t, dst_t, type_t, first_dst, rel_emb, w_msg, w_self, w1_l, w1_r,
                w2_l, w2_r, b_self, b_msg, b1, b2, x1_dram, h_dram, rdeg_dram, sum_dram, out):
    with ExitStack() as ctx:
        def sb(name, shape, dtype=F32):
            return ctx.enter_context(nc.sbuf_tensor(name, shape, dtype))

        def sem(name):
            return ctx.enter_context(nc.semaphore(name))

        A = sb("counts", [P, ROWS, WIDTH], F16)
        table0 = sb("table0", [P, ROWS, 2, D], F16)
        weights = sb("weights", [P, 6, D])
        bias = sb("bias", [33, 3, D])
        ident = sb("ident", [P, P])
        ones_h = sb("ones_h", [P, P], F16)
        eps_col = sb("eps_col", [P, 1])

        WORK = 7480
        work = sb("work", [P, WORK])

        def view(at, count, dtype=F32):
            words = count * (2 if dtype == F16 else 4) // 4
            assert at + words <= WORK, (at, words)
            piece = work[:, at:at + words]
            return (piece if dtype == F32 else piece.bitcast(dtype)), at + words

        at = 0
        iota_c, at = view(at, COMBINED, F16)
        iota_p, at = view(at, P, F16)
        PADDED = TILES + 2 * GROUP
        flat, at = view(at, PADDED * 4)
        edge_f = flat.rearrange("p (t k) -> p t k", k=4)
        combined_f, offset_f, type_f = (edge_f[:, 0:TILES, k] for k in (0, 2, 3))
        low_f = edge_f[:, :, 1]
        flat, at = view(at, DEPTH * GROUP)
        fetched = flat.rearrange("p (g t) -> p g t", g=DEPTH)
        base_i, at = view(at, GROUPS, I32)
        hot, at = view(at, DEPTH * GROUP * COMBINED, F16)
        M = hot.rearrange("p (g t c) -> p g t c", g=DEPTH, t=GROUP)
        hot, at = view(at, DEPTH * GROUP * P, F16)
        LOW = hot.rearrange("p (g t c) -> p g t c", g=DEPTH, t=GROUP)
        hot, at = view(at, DEPTH * GROUP * P, F16)
        TYPE = hot.rearrange("p (g t c) -> p g t c", g=DEPTH, t=GROUP)
        hot, at = view(at, 2 * GROUP * P, F16)
        DIST = hot.rearrange("p (g t c) -> p g t c", g=2, t=GROUP)
        hot, at = view(at, DEPTH * GROUP * WINDOW, F16)
        WIN = hot.rearrange("p (g t c) -> p g t c", g=DEPTH, t=GROUP)
        early_sum, at = view(at, CHUNK)
        build_end = at

        STAGED = 20
        stage = A[:, STAGED:ROWS, :].rearrange("p b w -> p (b w)").bitcast(F32)
        at = ROWS * D
        stage_x = stage[:, 0:at].rearrange("p (b d) -> p b d", d=D)

        def staged(at, count):
            return stage[:, at:at + count].bitcast(I32), at + count

        src_i, at = staged(at, TILES)
        dst_i, at = staged(at, TILES)
        type_i, at = staged(at, TILES)
        first_i, at = staged(at, GROUPS)
        block_i, at = staged(at, TILES)
        low_i, at = staged(at, TILES)
        off_middle = stage[:, at:at + TILES]
        floors = stage[:, at + TILES:at + TILES + GROUPS]

        at = 0
        second, at = view(at, BLOCKS * 2 * D, F16)
        table1 = second.rearrange("p (b s d) -> p b s d", b=BLOCKS, s=2)
        flat, at = view(at, CHUNK)
        residual = flat.rearrange("p (t d) -> p t d", t=SUB)
        own_T, at = view(at, CHUNK)
        rdeg, at = view(at, CHUNK)
        flat, at = view(at, SUB * 6)
        stats = flat.rearrange("p (t k) -> p t k", t=SUB)
        flat, at = view(at, SUB * 2)
        moments = flat.rearrange("p (t k) -> p t k", t=SUB)
        std, at = view(at, SUB)
        bias_rows_all, at = view(at, CHUNK)
        bias_rows = bias_rows_all[0:33, :]
        assert at >= build_end
        flat, at = view(at, 2 * CHUNK)
        own = flat.rearrange("p (s t d) -> p s t d", s=2, t=SUB)
        flat, at = view(at, 2 * CHUNK)
        mean_T = flat.rearrange("p (s n) -> p s n", s=2)
        peaks, at = view(at, PEAKS)
        limits, at = view(at, PEAKS)
        over, at = view(at, PEAKS)
        any_over, at = view(at, 1)
        ones_col, at = view(at, 1)
        flag, at = view(at, 1, I32)
        spare, at = view(at, 1)

        ps = ctx.enter_context(nc.psum_tensor("ps", [P, 8, 512], F32))
        DEG, DENSE, TURN = 4, 5, 7
        EARLY_HI, EARLY_LO = 4, 5

        edges_in = sem("edges_in")
        x_in = sem("x_in")
        weights_in = sem("weights_in")
        constants = sem("constants")
        pads_zero = sem("pads_zero")
        edge_step = sem("edge_step")
        scalars_ready = sem("scalars_ready")
        x_hi = sem("x_hi")
        x_rest = sem("x_rest")
        x_lo = sem("x_lo")
        zeroed = sem("zeroed")
        v_hot = sem("v_hot")
        p_hot = sem("p_hot")
        p_fetched = sem("p_fetched")
        a_dist = sem("a_dist")
        a_hot = sem("a_hot")
        counted = sem("counted")
        added = sem("added")
        bias_zero = sem("bias_zero")
        early_done = sem("early_done")
        early_scaled = sem("early_scaled")
        early_summed = sem("early_summed")
        early_stored = sem("early_stored")
        early_free = sem("early_free")
        sum_loaded = [sem(f"sum_loaded{k}") for k in range(2)]
        waited = sem("waited")
        over_step = sem("over_step")
        any_ready = sem("any_ready")
        over_counted = sem("over_counted")
        flag_ready = sem("flag_ready")
        work_zeroed = sem("work_zeroed")
        agg_done = sem("agg_done")
        deg_done = sem("deg_done")
        turned = sem("turned")
        dense_done = sem("dense_done")
        lo_scaled = sem("lo_scaled")
        own_T_ready = sem("own_T_ready")
        sigmoid_done = sem("sigmoid_done")
        std_ready = sem("std_ready")
        hi_ready = sem("hi_ready")
        lo_ready = sem("lo_ready")
        rdeg_step = sem("rdeg_step")
        rdeg_ready = sem("rdeg_ready")
        summed = sem("summed")
        mean_ready = sem("mean_ready")
        y_ready = sem("y_ready")
        ln_step = sem("ln_step")
        rows_ready = sem("rows_ready")
        rest_ready = sem("rest_ready")
        own_loaded = [sem(f"own_loaded{k}") for k in range(2)]
        residual_loaded = sem("residual_loaded")
        rdeg_loaded = sem("rdeg_loaded")
        rdeg_stored = sem("rdeg_stored")
        rows_stored = [sem(f"rows_stored{k}") for k in range(2)]

        IN_SLOT = [(CHUNKS + 1) // 2, CHUNKS // 2]

        def before(layer, half, slot):
            return layer * IN_SLOT[slot] + half

        def position(layer, half, slot):
            return layer * CHUNKS + half * 2 + slot

        def free(eng, semaphore, value):
            if not isinstance(value, int) or value > 0:
                eng.wait_ge(semaphore, value)

        def aggregated(layer, half, slot):
            return position(layer, half, slot) - EARLY

        def lead_and_post(eng, layer, lead, post, turn=None):
            turn = turn or (lambda *chunk: None)
            last = CHUNKS // 2
            lead(0, 0, CHUNK)
            turn(0, 0, CHUNK)

            def pair(half):
                for now, then in (((half, 1, CHUNK), (half, 0, CHUNK)),
                                  ((half + 1, 0, CHUNK), (half, 1, CHUNK))):
                    lead(*now)
                    post(*then)
                    turn(*now)

            pair(0)
            if layer == 0:
                for half in range(1, last - 1):
                    pair(half)
            else:
                with eng.Fori(1, last - 1) as half:
                    pair(half)
            lead(last - 1, 1, CHUNK)
            post(last - 1, 0, CHUNK)
            turn(last - 1, 1, CHUNK)
            lead(last, 0, LAST)
            post(last - 1, 1, CHUNK)
            turn(last, 0, LAST)
            post(last, 0, LAST)

        def nodes_at(half, slot, nodes):
            start = half * (2 * CHUNK) + slot * CHUNK
            return slice(start, start + nodes) if isinstance(start, int) else bass.ds(start, nodes)

        def dram_rows(dram, half, slot, nodes):
            rows = dram[nodes_at(half, slot, nodes), :]
            return rows if nodes == LAST else rows.rearrange("(t p) d -> p t d", p=P)

        def rows(buffer, nodes):
            return buffer[0:LAST, 0, :] if nodes == LAST else buffer

        def table_rows(table, half, slot, nodes, part):
            if nodes == LAST:
                return table[0:LAST, BLOCKS - 1, part, :]
            first = half * (2 * SUB) + slot * SUB
            span = slice(first, first + SUB) if isinstance(first, int) else bass.ds(first, SUB)
            return table[:, span, part, :]

        def dense_rows(bank, nodes):
            if nodes == LAST:
                return ps[0:LAST, bank, 0:D]
            return ps[:, bank, :].rearrange("p (t d) -> p t d", t=SUB)

        def column(tile):
            return slice(tile, tile + 1) if isinstance(tile, int) else bass.ds(tile, 1)

        def columns(tile):
            return slice(tile, tile + GROUP) if isinstance(tile, int) else bass.ds(tile, GROUP)

        def ln_chunks(layer, half, slot):
            return (0 if layer == 0 else CHUNKS) + half * 2 + slot

        def ln_steps(layer, half, slot):
            return ln_chunks(layer, half, slot) * 3

        free_words = A[:].rearrange("p b w -> p (b w)").bitcast(F32)

        def placed(at, count, dtype=F32):
            piece = free_words[:, at:at + count]
            return (piece if dtype == F32 else piece.bitcast(dtype)), at + count

        g_iota, at = placed(0, N)
        g_hot, at = placed(at, N)
        g_mean_T, at = placed(at, N)
        g_rdeg, at = placed(at, N)
        g_rows_of_bias, at = placed(at, N)
        g_bias_rows = g_rows_of_bias[0:33]
        g_src, at = placed(at, TILES, I32)
        g_dst, at = placed(at, TILES, I32)
        g_type, at = placed(at, TILES, I32)
        g_dst_f, at = placed(at, TILES)
        g_index, at = placed(at, 2, I32)
        g_ones, at = placed(at, P)
        g_source, at = placed(at, D)
        g_relation, at = placed(at, D)
        g_own, at = placed(at, D)
        g_residual, at = placed(at, D)
        g_own_T, at = placed(at, P)
        g_mean_tile, at = placed(at, P)
        g_bias_tile, at = placed(at, P)
        g_sigmoid, at = placed(at, D)
        g_new, at = placed(at, D)
        g_stats, at = placed(at, 6)
        g_moments, at = placed(at, 2)
        g_std, at = placed(at, 1)
        G_TURN, G_DENSE = slice(0, P), slice(P, P + D)

        gs_edges = sem("general_edges")
        gs_setup = sem("general_setup")
        gs_lists = sem("general_lists")
        gs_index = sem("general_index")
        gs_source = sem("general_source")
        gs_relation = sem("general_relation")
        gs_message = sem("general_message")
        gs_hot = sem("general_hot")
        gs_counted = sem("general_counted")
        gs_pass = sem("general_pass")
        gs_own = sem("general_own")
        gs_turned = sem("general_turned")
        gs_own_T = sem("general_own_T")
        gs_dense = sem("general_dense")
        gs_sigmoid = sem("general_sigmoid")
        gs_std = sem("general_std")
        gs_step = sem("general_step")
        gs_row = sem("general_row")
        gs_stored = sem("general_stored")

        def hold(eng, semaphore, value):
            if not isinstance(value, int) or value > 0:
                eng.wait_ge(semaphore, value)
                eng.sem_inc(waited, 1)

        def if_over(eng, engine_type, general):
            eng.wait_ge(flag_ready, 1)
            found = nc.values_load_multi_w_load_instructions(
                flag[0:1, 0:1], engines=[engine_type], min_val=0, max_val=P,
                skip_runtime_bounds_check_because="it counts partitions")[1][0]
            with eng.If(found != 0):
                for slot in range(2):
                    eng.wait_ge(rows_stored[slot], 16 * before(3, 0, slot))
                eng.sem_inc(waited, 1)
                general()

        def edge_tiles(eng, step):
            step(0, True)
            with eng.Fori(1, TILES) as tile:
                step(tile, False)

        def node_tiles(eng, step):
            step(0, P)
            with eng.Fori(1, BLOCKS - 1) as tile:
                step(tile, P)
            step(BLOCKS - 1, N - P * (BLOCKS - 1))

        def node_span(tile, size):
            return slice(tile * P, tile * P + size) if isinstance(tile, int) else bass.ds(
                tile * P, size)

        def general_sync(sp):
            def general():
                for to, given in ((g_src, src_t), (g_dst, dst_t), (g_type, type_t)):
                    sp.dma_start(to, given).then_inc(gs_edges, 16)
                for layer, (source, sink) in enumerate(((x, x1_dram), (x1_dram, h_dram),
                                                        (h_dram, out))):
                    def step(tile, size, layer=layer, source=source, sink=sink):
                        q = layer * BLOCKS + tile
                        span = node_span(tile, size)
                        hold(sp, gs_stored, q * 16)
                        sp.dma_start(g_own[0:size], source[span, :]).then_inc(gs_own, 16)
                        sp.dma_start(g_residual[0:size], (x1_dram if layer == 2 else source)
                                     [span, :]).then_inc(gs_own, 16)
                        hold(sp, gs_row, q + 1)
                        sp.dma_start(sink[span, :], g_new[0:size]).then_inc(gs_stored, 16)

                    node_tiles(sp, step)
                sp.wait_ge(gs_stored, 16 * 3 * BLOCKS)

            if_over(sp, mybir.EngineType.SP, general)

        def general_gpsimd(pool):
            def general():
                nc.gpsimd.iota(g_iota, [[1, N]], base=0, channel_multiplier=0,
                               allow_small_or_imprecise_dtypes=True).then_inc(gs_setup, 1)
                nc.gpsimd.memset(g_ones, 1.0).then_inc(gs_setup, 1)
                nc.gpsimd.memset(g_rows_of_bias, 0.0).then_inc(gs_setup, 1)
                pool.wait_ge(gs_setup, 3)
                nc.gpsimd.memset(g_rows_of_bias[0:1], 1.0).then_inc(gs_setup, 1)
                pool.wait_ge(gs_lists, 1)
                for layer, source in enumerate((x, x1_dram, h_dram)):
                    hold(pool, gs_stored, 16 * BLOCKS * layer)

                    def step(tile, _, layer=layer, source=source):
                        n = layer * TILES + tile
                        hold(pool, gs_counted, n + TILES)
                        nc.gpsimd.tensor_copy(g_index[:, 0:1], g_src[:, column(tile)]
                                              ).then_inc(gs_index, 1)
                        nc.gpsimd.tensor_copy(g_index[:, 1:2], g_type[:, column(tile)]
                                              ).then_inc(gs_index, 1)
                        hold(pool, gs_index, 2 * n + 2)
                        nc.gpsimd.indirect_dma_start(
                            g_source, None, source,
                            bass.IndirectOffsetOnAxis(ap=g_index[:, 0:1], axis=0)
                        ).then_inc(gs_source, 16)
                        if layer == 0:
                            nc.gpsimd.indirect_dma_start(
                                g_relation, None, rel_emb,
                                bass.IndirectOffsetOnAxis(ap=g_index[:, 1:2], axis=0)
                            ).then_inc(gs_relation, 16)

                    edge_tiles(pool, step)

            if_over(pool, mybir.EngineType.Pool, general)

        def general_scalar(act):
            def general():
                for layer in range(3):
                    act.wait_ge(gs_pass, layer + 2)

                    def step(tile, size, layer=layer):
                        q = layer * BLOCKS + tile
                        span = node_span(tile, size)
                        hold(act, gs_turned, q + 1)
                        nc.scalar.copy(g_mean_tile[:, 0:size], g_mean_T[:, span])
                        nc.scalar.copy(g_bias_tile[0:33, 0:size], g_bias_rows[:, span])
                        nc.scalar.copy(g_own_T[:, 0:size], ps[:, 7, 0:size]
                                       ).then_inc(gs_own_T, 1)
                        if layer == 1:
                            hold(act, gs_dense, q + 1)
                            nc.scalar.activation(g_sigmoid[0:size], ps[0:size, 7, G_DENSE],
                                                 ACT.Sigmoid).then_inc(gs_sigmoid, 1)
                        else:
                            normalised = (0 if layer == 0 else BLOCKS) + tile
                            hold(act, gs_step, normalised * 4 + 3)
                            nc.scalar.activation(g_std[0:size], g_moments[0:size, 1:2],
                                                 ACT.Sqrt, bias=eps_col[0:size]
                                                 ).then_inc(gs_std, 1)

                    node_tiles(act, step)

            if_over(act, mybir.EngineType.Activation, general)

        def general_tensor(pe):
            def general():
                pe.wait_ge(gs_setup, 4)
                for k in range(4):
                    hold(pe, gs_pass, k)
                    hold(pe, gs_row, BLOCKS * (k - 1))

                    def step(tile, first, k=k):
                        hold(pe, gs_hot, k * TILES + tile + 1)
                        if k == 1:
                            hold(pe, gs_message, tile + 1)
                        elif k > 1:
                            hold(pe, gs_source, ((k - 1) * TILES + tile) * 16 + 16)
                        for c in range(CHUNKS):
                            nodes = CHUNK if c < CHUNKS - 1 else LAST
                            last = nc.tensor.matmul(
                                ps[:, c, 0:nodes], g_source if k else g_ones,
                                g_hot[:, c * CHUNK:c * CHUNK + nodes],
                                start=first, stop=not first, skip_group_check=True)
                        last.then_inc(gs_counted, 1)

                    edge_tiles(pe, step)
                    if k == 0:
                        continue
                    hold(pe, gs_pass, k + 1)

                    def dense(tile, size, layer=k - 1):
                        q = layer * BLOCKS + tile
                        hold(pe, gs_own, q * 32 + 32)
                        nc.tensor.transpose(ps[:, 7, 0:size], g_own[0:size],
                                            ident[0:size, 0:size]).then_inc(gs_turned, 1)
                        hold(pe, gs_own_T, q + 1)
                        to = ps[0:size, 7, G_DENSE]
                        keep = 33 if layer == 0 else 1
                        nc.tensor.matmul(to, g_mean_tile[:, 0:size],
                                         weights[:, 2 * layer, :], start=True, stop=False)
                        nc.tensor.matmul(to, g_own_T[:, 0:size], weights[:, 2 * layer + 1, :],
                                         start=False, stop=False)
                        nc.tensor.matmul(to, g_bias_tile[0:keep, 0:size],
                                         bias[0:keep, layer, :],
                                         start=False, stop=True).then_inc(gs_dense, 1)

                    node_tiles(pe, dense)

            if_over(pe, mybir.EngineType.PE, general)

        def general_vector(dve):
            def general():
                dve.wait_ge(gs_edges, 48)
                nc.vector.tensor_copy(g_dst_f, g_dst)
                nc.vector.tensor_scalar(g_type, g_type, 0, RELATIONS - 1, ALU.max, ALU.min
                                        ).then_inc(gs_lists, 1)
                dve.wait_ge(gs_lists, 1)
                dve.wait_ge(gs_setup, 4)
                sums = ps[:].rearrange("p b c -> p (b c)")[:, 0:N]
                for k in range(4):
                    def step(tile, _, k=k):
                        n = k * TILES + tile
                        hold(dve, gs_counted, n)
                        nc.vector.tensor_scalar(g_hot, g_iota, g_dst_f[:, column(tile)], None,
                                                ALU.is_equal).then_inc(gs_hot, 1)
                        if k == 1:
                            hold(dve, gs_source, tile * 16 + 16)
                            hold(dve, gs_relation, tile * 16 + 16)
                            nc.vector.tensor_tensor(g_source, g_source, g_relation, ALU.add
                                                    ).then_inc(gs_message, 1)

                    edge_tiles(dve, step)
                    hold(dve, gs_counted, (k + 1) * TILES)
                    if k == 0:
                        nc.vector.tensor_scalar(g_rdeg, sums, 1.0, None, ALU.max)
                        nc.vector.tensor_scalar(g_bias_rows[32:33], sums[32:33], 1.0, None,
                                                ALU.min).then_inc(gs_lists, 1)
                        dve.wait_ge(gs_lists, 2)
                        nc.vector.reciprocal(g_rdeg, g_rdeg).then_inc(gs_pass, 1)
                        dve.wait_ge(gs_pass, 1)
                        continue
                    nc.vector.tensor_tensor(g_mean_T, sums, g_rdeg, ALU.mult
                                            ).then_inc(gs_pass, 1)

                    def rows_of(tile, size, layer=k - 1):
                        q = layer * BLOCKS + tile
                        y = g_new[0:size]
                        products = ps[0:size, 7, G_DENSE]
                        if layer == 1:
                            hold(dve, gs_sigmoid, tile + 1)
                            nc.vector.tensor_tensor(y, products, g_sigmoid[0:size], ALU.mult
                                                    ).then_inc(gs_row, 1)
                            return
                        done = ((0 if layer == 0 else BLOCKS) + tile) * 4
                        hold(dve, gs_dense, q + 1)
                        nc.vector.tensor_tensor(y, products, g_residual[0:size], ALU.add
                                                ).then_inc(gs_step, 1)
                        hold(dve, gs_step, done + 1)
                        nc.vector.bn_stats(g_stats[0:size], y).then_inc(gs_step, 1)
                        hold(dve, gs_step, done + 2)
                        nc.vector.bn_aggr(g_moments[0:size], g_stats[0:size]
                                          ).then_inc(gs_step, 1)
                        hold(dve, gs_std, (0 if layer == 0 else BLOCKS) + tile + 1)
                        nc.vector.reciprocal(g_std[0:size], g_std[0:size]
                                             ).then_inc(gs_step, 1)
                        hold(dve, gs_step, done + 4)
                        nc.vector.tensor_scalar(y, y, g_moments[0:size, 0:1], g_std[0:size],
                                                ALU.subtract, ALU.mult).then_inc(gs_row, 1)

                    node_tiles(dve, rows_of)

            if_over(dve, mybir.EngineType.DVE, general)

        def build(group_pair, early_start=None, early_block=None, early_end=None, eng=None):
            with eng.Fori(0, LEAD // DEPTH) as i:
                group_pair(i * DEPTH, None)

            def period(k, length):
                if early_start:
                    early_start(k)
                first = k * PERIOD + LEAD
                with eng.Fori(0, STEPS) as i:
                    group_pair(first + i * DEPTH,
                               early_block and (lambda j: early_block(k, i * DEPTH + (1 + j))))
                group_pair(first + EARLY_DONE, None)
                if early_end:
                    early_end(k)
                with eng.Fori(1, (length - EARLY_DONE) // DEPTH) as i:
                    group_pair(first + EARLY_DONE + i * DEPTH, None)

            with eng.Fori(0, EARLY - 1) as k:
                period(k, PERIOD)
            period(EARLY - 1, GROUPS - LEAD - PERIOD * (EARLY - 1))

        block = ctx.enter_context(nc.Block())

        @block.sync
        def _(sp):
            sp.dma_start(dst_i, dst_t).then_inc(edges_in, 16)
            sp.dma_start(first_i, first_dst.partition_broadcast(P)).then_inc(edges_in, 16)
            sp.dma_start(src_i, src_t).then_inc(edges_in, 16)
            sp.dma_start(type_i, type_t).then_inc(edges_in, 16)
            full = (BLOCKS - 1) * P
            sp.wait_ge(pads_zero, 1)
            sp.dma_start(stage_x[:, 0:BLOCKS - 1, :],
                         x[0:full, :].rearrange("(b p) d -> p b d", p=P)).then_inc(x_in, 16)
            sp.dma_start(stage_x[0:N - full, BLOCKS - 1, :], x[full:N, :]).then_inc(x_in, 16)
            sp.dma_start(stage_x[0:RELATIONS, BLOCKS, :], rel_emb).then_inc(x_in, 16)
            sp.wait_ge(constants, 1)
            for k, w in enumerate((w_msg, w_self, w1_l, w1_r, w2_l, w2_r)):
                sp.dma_start(weights[:, k, :], w).then_inc(weights_in, 16)
            for row, k, b in ((0, 0, b_self), (32, 0, b_msg), (0, 1, b1), (0, 2, b2)):
                sp.dma_start(bias[row:row + 1, k, :], b).then_inc(weights_in, 16)

            with sp.Fori(0, EARLY) as k:
                sp.wait_ge(early_summed, k + 2)
                sp.sem_inc(waited, 1)
                sp.dma_start(sum_dram[:, bass.ds(k * CHUNK, CHUNK)], early_sum
                             ).then_inc(early_stored, 16)
                sp.wait_ge(early_stored, k * 16 + 16)
                sp.sem_inc(early_free, 1)

            for layer, (source, sink) in enumerate(((x, x1_dram), (x1_dram, h_dram),
                                                    (h_dram, out))):
                def load(half, slot, nodes, layer=layer, source=source):
                    free(sp, rows_stored[slot], before(layer, half, slot) * 16)
                    sp.sem_inc(waited, 1)
                    q = position(layer, half, slot)
                    first = isinstance(half, int) and half == 0
                    if layer < 2:
                        used = q if layer and slot == 0 and first else q - 1
                        free(sp, hi_ready, used)
                        free(sp, rest_ready, used)
                    elif first:
                        sp.wait_ge(hi_ready, 2 * CHUNKS)
                        sp.wait_ge(rest_ready, 2 * CHUNKS)
                    sp.dma_start(rows(own[:, slot], nodes), dram_rows(source, half, slot, nodes)
                                 ).then_inc(own_loaded[slot], 16)

                def store(half, slot, nodes, layer=layer, sink=sink):
                    sp.wait_ge(rows_ready, position(layer, half, slot) + 1)
                    sp.dma_start(dram_rows(sink, half, slot, nodes), rows(own[:, slot], nodes)
                                 ).then_inc(rows_stored[slot], 16)

                def load_residual(half, slot, nodes):
                    sp.dma_start(rows(residual, nodes), dram_rows(x1_dram, half, slot, nodes)
                                 ).then_inc(residual_loaded, 16)

                load(0, 0, CHUNK)
                load(0, 1, CHUNK)
                if layer == 2:
                    load_residual(0, 0, CHUNK)
                with sp.Fori(0, 2) as half:
                    for slot in range(2):
                        store(half, slot, CHUNK)
                        if layer == 2:
                            load_residual(*((half, 1) if slot == 0 else (half + 1, 0)), CHUNK)
                        load(half + 1, slot, CHUNK)
                store(2, 0, CHUNK)
                if layer == 2:
                    load_residual(2, 1, CHUNK)
                load(3, 0, LAST)
                store(2, 1, CHUNK)
                if layer == 2:
                    load_residual(3, 0, LAST)
                store(3, 0, LAST)
            for slot in range(2):
                sp.wait_ge(rows_stored[slot], 16 * before(3, 0, slot))
            general_sync(sp)

        @block.gpsimd
        def _(pool):
            nc.gpsimd.memset(bias[:], 0.0).then_inc(constants, 1)
            nc.gpsimd.iota(iota_c, [[1, COMBINED]], base=0, channel_multiplier=0,
                           allow_small_or_imprecise_dtypes=True).then_inc(constants, 1)
            nc.gpsimd.iota(iota_p, [[1, P]], base=0, channel_multiplier=0,
                           allow_small_or_imprecise_dtypes=True).then_inc(constants, 1)
            nc.gpsimd.memset(ones_h[:], 1.0).then_inc(constants, 1)
            nc.gpsimd.memset(eps_col[:], EPS).then_inc(constants, 1)
            nc.gpsimd.memset(ident[:], 0.0).then_inc(constants, 1)
            nc.gpsimd.memset(ones_col, 1.0).then_inc(constants, 1)
            pool.wait_ge(constants, 7)
            nc.gpsimd.affine_select(out=ident[:], in_=ident[:], compare_op=ALU.not_equal,
                                    fill=1.0, base=0, pattern=[[-1, P]],
                                    channel_multiplier=1).then_inc(constants, 1)
            for b in range(7, 13):
                nc.gpsimd.memset(A[:, b, :].bitcast(U32), 0).then_inc(zeroed, 1)
            pool.wait_ge(scalars_ready, 1)
            pool.wait_ge(x_lo, 1)
            for b in (24, 25):
                nc.gpsimd.memset(A[:, b, :].bitcast(U32), 0).then_inc(zeroed, 1)

            def fetch(group, slot):
                nc.gpsimd.tensor_copy(fetched[:, slot], low_f[:, columns(group * GROUP)]
                                      ).then_inc(p_fetched, 1)

            def one_hots(group, slot):
                pool.wait_ge(p_fetched, group + 1)
                pool.wait_ge(p_hot, group + 1)
                fetch(group + 1, 1 - slot)
                for t in range(GROUP):
                    last = nc.gpsimd.tensor_scalar(LOW[:, slot, t], iota_p,
                                                   fetched[:, slot, t:t + 1], None, ALU.is_equal)
                last.then_inc(p_hot, 1)

            pool.sem_inc(p_hot, 1)
            fetch(0, 0)
            one_hots(0, 0)
            one_hots(1, 1)
            with pool.Fori(0, GROUPS // DEPTH - 1) as i:
                for j in range(DEPTH):
                    pool.wait_ge(counted, i * DEPTH + (j + 1))
                    one_hots(i * DEPTH + (DEPTH + j), j)

            pool.wait_ge(early_stored, 16 * EARLY)

            def load_sum(chunk):
                half, slot = divmod(chunk, 2)
                free(pool, dense_done, chunk - 1)
                free(pool, lo_ready, chunk - 1)
                pool.dma_start(mean_T[:, slot], sum_dram[:, nodes_at(half, slot, CHUNK)]
                               ).then_inc(sum_loaded[slot], 16)

            load_sum(0)
            load_sum(1)
            for chunk in range(CHUNKS):
                nodes = CHUNK if chunk < CHUNKS - 1 else LAST
                pool.wait_ge(rdeg_ready, chunk + 1)
                pool.dma_start(rdeg_dram[:, nodes_at(chunk // 2, chunk % 2, nodes)],
                               rdeg[:, 0:nodes]).then_inc(rdeg_stored, 16)
                if 2 <= chunk + 1 < EARLY:
                    load_sum(chunk + 1)
            pool.wait_ge(rdeg_stored, 16 * CHUNKS)
            for layer in (1, 2):
                def load_rdeg(half, slot, nodes, layer=layer):
                    pool.wait_ge(mean_ready, position(layer, half, slot))
                    pool.dma_start(rdeg[:, 0:nodes], rdeg_dram[:, nodes_at(half, slot, nodes)]
                                   ).then_inc(rdeg_loaded, 16)

                with pool.Fori(0, 3) as half:
                    load_rdeg(half, 0, CHUNK)
                    load_rdeg(half, 1, CHUNK)
                load_rdeg(3, 0, LAST)
            general_gpsimd(pool)

        @block.scalar
        def _(act):
            for b in range(7):
                nc.scalar.memzero(A[:, b, :].bitcast(U32)).then_inc(zeroed, 1)
            act.wait_ge(x_in, 48)
            nc.scalar.activation(table0[:, :, 0, :], stage_x, ACT.Copy).then_inc(x_hi, 1)
            act.wait_ge(x_rest, 1)
            nc.scalar.activation(table0[:, :, 1, :], stage_x, ACT.Copy, scale=SPLIT
                                 ).then_inc(x_lo, 1)
            act.wait_ge(x_lo, 1)
            act.wait_ge(scalars_ready, 1)
            for b in (22, 23):
                nc.scalar.memzero(A[:, b, :].bitcast(U32)).then_inc(zeroed, 1)

            def one_hots(group, slot):
                tile = group * GROUP
                for t in range(GROUP):
                    last = nc.scalar.activation(DIST[:, slot, t], iota_p, ACT.Abs, scale=-1.0,
                                                bias=edge_f[:, column(tile + t), 3])
                last.then_inc(a_dist, 1)
                act.wait_ge(a_dist, group + 1)
                nc.scalar.activation(TYPE[:, slot], DIST[:, slot], ACT.Relu, scale=-1.0,
                                     bias=1.0).then_inc(a_hot, 1)

            def group_pair(first, _):
                for j in range(DEPTH):
                    act.wait_ge(added, first + (j + 1))
                    act.wait_ge(a_hot, first + (j + 1))
                    one_hots(first + j, j)

            def early_end(k):
                act.wait_ge(early_done, k + 1)
                act.wait_ge(early_free, k + 1)
                nc.scalar.activation(early_sum, ps[:, EARLY_LO], ACT.Copy, scale=1.0 / SPLIT
                                     ).then_inc(early_scaled, 1)

            act.sem_inc(a_hot, 2)
            build(group_pair, early_end=early_end, eng=act)

            act.wait_ge(added, GROUPS + 2)
            for layer in range(3):
                to_table = (table1, table0, None)[layer]

                def lead(half, slot, nodes, layer=layer):
                    q = position(layer, half, slot)
                    if layer or 2 * half + slot >= EARLY:
                        act.wait_ge(agg_done, aggregated(layer, half, slot) + 1)
                        act.wait_ge(dense_done, q - 1)
                        act.wait_ge(lo_ready, q - 1 if layer < 2 else 2 * CHUNKS)
                        nc.scalar.activation(mean_T[:, slot, 0:nodes],
                                             ps[:, 2 * slot + 1, 0:nodes], ACT.Copy,
                                             scale=1.0 / SPLIT).then_inc(lo_scaled, 1)
                    act.wait_ge(turned, q + 1)
                    free(act, dense_done, q)
                    nc.scalar.copy(own_T[:, 0:nodes], ps[:, TURN, 0:nodes]
                                   ).then_inc(own_T_ready, 1)

                def post(half, slot, nodes, layer=layer, to_table=to_table):
                    q = position(layer, half, slot)
                    part = LAST if nodes == LAST else P
                    count = 1 if nodes == LAST else SUB
                    scratch = mean_T[:, slot].rearrange("p (t d) -> p t d", t=SUB)
                    if layer == 1:
                        act.wait_ge(dense_done, q + 1)
                        nc.scalar.activation(rows(scratch, nodes),
                                             dense_rows(DENSE + slot, nodes), ACT.Sigmoid
                                             ).then_inc(sigmoid_done, 1)
                    else:
                        act.wait_ge(ln_step, ln_steps(layer, half, slot) + 2)
                        free(act, rows_ready, q)
                        nc.scalar.activation(std[0:part, 0:count], moments[0:part, 0:count, 1],
                                             ACT.Sqrt, bias=eps_col[0:part]
                                             ).then_inc(std_ready, 1)
                    if layer < 2:
                        act.wait_ge(rows_ready, q + 1)
                        nc.scalar.activation(table_rows(to_table, half, slot, nodes, 0),
                                             rows(own[:, slot], nodes), ACT.Copy
                                             ).then_inc(hi_ready, 1)
                        act.wait_ge(rest_ready, q + 1)
                        nc.scalar.activation(table_rows(to_table, half, slot, nodes, 1),
                                             rows(scratch, nodes), ACT.Copy, scale=SPLIT
                                             ).then_inc(lo_ready, 1)

                lead_and_post(act, layer, lead, post)
            general_scalar(act)

        @block.tensor
        def _(pe):
            def count(group, slot):
                pe.wait_ge(v_hot, group + 1)
                pe.wait_ge(p_hot, group + 2)
                pe.wait_ge(a_hot, group + 3)
                pe.wait_ge(added, group + 1)
                cut = HALF * WINDOW
                low, high = 2 * slot, 2 * slot + 1
                for t in range(GROUP):
                    first = t == 0
                    nc.tensor.matmul(ps[:, low, 0:cut], LOW[:, slot, t], M[:, slot, t, 0:cut],
                                     start=first, stop=not first, skip_group_check=True)
                    nc.tensor.matmul(ps[:, high, 0:COMBINED - cut], LOW[:, slot, t],
                                     M[:, slot, t, cut:COMBINED],
                                     start=first, stop=not first, skip_group_check=True)
                    last = nc.tensor.matmul(ps[:, high, COMBINED - cut:cut],
                                            TYPE[:, slot, t], WIN[:, slot, t],
                                            start=False, stop=not first, skip_group_check=True)
                last.then_inc(counted, 1)

            def multiply(b, chunk_at):
                edge = isinstance(b, int)
                for part, bank in ((0, EARLY_HI), (1, EARLY_LO)):
                    block_at = b if edge else bass.ds(b, 1)
                    stationary = table0[:, block_at, part, :]
                    moving = A[:, block_at, chunk_at]
                    if not edge:
                        stationary, moving = stationary.squeeze(1), moving.squeeze(1)
                    last = nc.tensor.matmul(ps[:, bank, :], stationary, moving,
                                            start=edge and b == 0, stop=edge and b > 0,
                                            skip_group_check=True)
                return last

            def early_start(k):
                pe.wait_ge(early_summed, k + 1)
                multiply(0, columns_of(k))

            def early_end(k):
                multiply(ROWS - 1, columns_of(k)).then_inc(early_done, 1)

            def columns_of(k):
                return bass.ds(k * CHUNK, CHUNK) if not isinstance(k, int) else slice(
                    k * CHUNK, (k + 1) * CHUNK)

            def group_pair(first, early_block):
                for j in range(DEPTH):
                    count(first + j, j)
                    if early_block:
                        early_block(j)

            pe.wait_ge(x_lo, 1)
            build(group_pair, early_start, lambda k, b: multiply(b, columns_of(k)), early_end,
                  eng=pe)

            pe.wait_ge(added, GROUPS + 2)
            pe.wait_ge(early_summed, EARLY + 1)
            pe.wait_ge(constants, 8)
            pe.wait_ge(weights_in, 16 * 10)

            def aggregate(layer, half, slot, nodes):
                table = (table0, table1, table0)[layer]
                blocks = ROWS if layer == 0 else BLOCKS
                at = nodes_at(half, slot, nodes)
                for part in range(2):
                    for b in range(blocks):
                        last = nc.tensor.matmul(ps[:, 2 * slot + part, 0:nodes],
                                                table[:, b, part, :], A[:, b, at],
                                                start=b == 0, stop=b == blocks - 1)
                last.then_inc(agg_done, 1)

            for chunk in range(EARLY, CHUNKS):
                aggregate(0, chunk // 2, chunk % 2, CHUNK if chunk < CHUNKS - 1 else LAST)
            pe.wait_ge(work_zeroed, 1)
            for layer in range(3):
                if layer:
                    pe.wait_ge(lo_ready, layer * CHUNKS)

                def lead(half, slot, nodes, layer=layer):
                    q = position(layer, half, slot)
                    if layer:
                        pe.wait_ge(summed, aggregated(layer, half, slot) - 1)
                        aggregate(layer, half, slot, nodes)
                    else:
                        free(pe, rdeg_ready, q)
                        nc.tensor.matmul(ps[:, DEG, 0:nodes], ones_h[:],
                                         A[:, BLOCKS, nodes_at(half, slot, nodes)],
                                         start=True, stop=True).then_inc(deg_done, 1)

                def turn(half, slot, nodes, layer=layer):
                    pe.wait_ge(own_loaded[slot], before(layer, half, slot) * 16 + 16)
                    free(pe, own_T_ready, position(layer, half, slot))
                    for t in range(1 if nodes == LAST else SUB):
                        size = min(P, nodes)
                        last = nc.tensor.transpose(ps[:, TURN, t * P:t * P + size],
                                                   own[0:size, slot, t, :],
                                                   ident[0:size, 0:size])
                    last.then_inc(turned, 1)

                def post(half, slot, nodes, layer=layer):
                    q = position(layer, half, slot)
                    pe.wait_ge(mean_ready, q + 1)
                    pe.wait_ge(own_T_ready, q + 1)
                    pe.wait_ge(y_ready, q + 1)
                    keep = 33 if layer == 0 else 1
                    for t in range(1 if nodes == LAST else SUB):
                        size = min(P, nodes)
                        at = slice(t * P, t * P + size)
                        to = ps[0:size, DENSE + slot, t * D:(t + 1) * D]
                        nc.tensor.matmul(to, mean_T[:, slot, at], weights[:, 2 * layer, :],
                                         start=True, stop=False)
                        nc.tensor.matmul(to, own_T[:, at], weights[:, 2 * layer + 1, :],
                                         start=False, stop=False)
                        last = nc.tensor.matmul(to, bias_rows[0:keep, at],
                                                bias[0:keep, layer, :],
                                                start=False, stop=True)
                    last.then_inc(dense_done, 1)

                if layer == 2:
                    pe.wait_ge(any_ready, 1)
                    nc.tensor.matmul(ps[0:1, DEG, 0:1], any_over, ones_col,
                                     start=True, stop=True).then_inc(over_counted, 1)
                lead_and_post(pe, layer, lead, post, turn)
            general_tensor(pe)

        @block.vector
        def _(dve):
            nc.vector.memset(stage_x[:, BLOCKS - 1:ROWS, :], 0.0).then_inc(pads_zero, 1)
            nc.vector.memset(edge_f[:, TILES:PADDED, :], -1.0)
            nc.vector.memset(peaks, 0.0)
            nc.vector.memset(limits[:, 0:1], (WINDOW - 1) / 2)
            nc.vector.memset(limits[:, 1:2], 0.0)
            nc.vector.memset(limits[:, 2:3], MOST_VALUE)
            nc.vector.memset(limits[:, 3:3 + CHUNKS], MOST_EDGES - 1)
            nc.vector.memset(limits[:, 3 + CHUNKS:PEAKS], MOST_VALUE)
            nc.vector.memset(off_middle[:, FULL_TILES:TILES], 0.0)
            nc.vector.memset(floors[:, 0:LEAD - DEPTH], -1.0)
            for k in range(EARLY):
                end = LEAD - DEPTH + (k + 1) * PERIOD if k < EARLY - 1 else GROUPS
                nc.vector.memset(floors[:, LEAD - DEPTH + k * PERIOD:end], float(CHUNK * (k + 1)))
            nc.vector.memset(spare, 0.0).then_inc(edge_step, 1)
            for b in range(13, STAGED):
                nc.vector.memset(A[:, b, :].bitcast(U32), 0).then_inc(zeroed, 1)

            dve.wait_ge(edges_in, 64)
            dve.wait_ge(edge_step, 1)
            nc.vector.tensor_scalar(low_i, src_i, P - 1, None, ALU.bitwise_and
                                    ).then_inc(edge_step, 1)
            nc.vector.tensor_scalar(block_i, src_i, P.bit_length() - 1, None,
                                    ALU.arith_shift_right).then_inc(edge_step, 1)
            nc.vector.tensor_tensor(offset_f.rearrange("p (g t) -> p g t", t=GROUP),
                                    dst_i.rearrange("p (g t) -> p g t", t=GROUP),
                                    first_i.unsqueeze(2).to_broadcast([P, GROUPS, GROUP]),
                                    ALU.subtract).then_inc(edge_step, 1)
            nc.vector.tensor_scalar(type_f, type_i, 0, RELATIONS - 1, ALU.max, ALU.min
                                    ).then_inc(edge_step, 1)
            nc.vector.tensor_tensor(base_i, floors, first_i, ALU.max).then_inc(edge_step, 1)
            dve.wait_ge(edge_step, 6)
            nc.vector.tensor_copy(low_f[:, 0:TILES], low_i).then_inc(edge_step, 1)
            nc.vector.scalar_tensor_tensor(combined_f, block_i, float(WINDOW), offset_f,
                                           ALU.mult, ALU.add).then_inc(edge_step, 1)
            middle = -(WINDOW - 1) / 2
            nc.vector.tensor_scalar(off_middle[:, 0:FULL_TILES], offset_f[:, 0:FULL_TILES],
                                    middle, None, ALU.add).then_inc(edge_step, 1)
            rest = E - FULL_TILES * P
            nc.vector.tensor_scalar(off_middle[0:rest, FULL_TILES:TILES],
                                    offset_f[0:rest, FULL_TILES:TILES],
                                    middle, None, ALU.add).then_inc(edge_step, 1)
            nc.vector.tensor_tensor(floors, floors, first_i, ALU.subtract
                                    ).then_inc(edge_step, 1)
            dve.wait_ge(edge_step, 11)
            nc.vector.tensor_reduce(peaks[:, 0:1], off_middle, AX.X, ALU.max,
                                    apply_absolute_value=True)
            nc.vector.tensor_reduce(peaks[:, 1:2], floors, AX.X, ALU.max
                                    ).then_inc(edge_step, 1)
            dve.wait_ge(edge_step, 12)
            dve.wait_ge(constants, 8)
            nc.vector.engine_nop().then_inc(scalars_ready, 1)
            dve.wait_ge(x_in, 48)
            nc.vector.tensor_reduce(peaks[:, 2:3], stage_x, AX.XY, ALU.max,
                                    apply_absolute_value=True).then_inc(edge_step, 1)
            dve.wait_ge(edge_step, 13)
            dve.wait_ge(x_hi, 1)
            nc.vector.tensor_tensor(stage_x, stage_x, table0[:, :, 0, :], ALU.subtract
                                    ).then_inc(x_rest, 1)
            dve.wait_ge(x_lo, 1)
            for b in (20, 21):
                nc.vector.memset(A[:, b, :].bitcast(U32), 0).then_inc(zeroed, 1)

            def one_hots(group, slot):
                tile = group * GROUP
                nc.vector.tensor_tensor(
                    WIN[:, slot],
                    iota_p[:, 0:WINDOW].unsqueeze(1).to_broadcast([P, GROUP, WINDOW]),
                    edge_f[:, columns(tile), 2:3].to_broadcast([P, GROUP, WINDOW]),
                    ALU.is_equal)
                for t in range(GROUP):
                    last = nc.vector.tensor_scalar(M[:, slot, t], iota_c,
                                                   edge_f[:, column(tile + t), 0],
                                                   None, ALU.is_equal)
                last.then_inc(v_hot, 1)

            def add(group, slot, base):
                dve.wait_ge(counted, group + 1)
                dve.wait_ge(added, group + 2)
                window = A[:, :, bass.ds(base, WINDOW)].rearrange("p (a b) w -> p a b w", a=2)
                counts = ps[:, 2 * slot:2 * slot + 2, 0:HALF * WINDOW].rearrange(
                    "p a (b w) -> p a b w", w=WINDOW)
                nc.vector.tensor_tensor(window, counts, window, ALU.add).then_inc(added, 1)

            def group_pair(first, _):
                base = nc.values_load_multi_w_load_instructions(
                    base_i[0:1, bass.ds(first, DEPTH)], engines=[DVE], min_val=0, max_val=N - 1,
                    skip_runtime_bounds_check_because="node numbers are below N")[1]
                for j in range(DEPTH):
                    one_hots(first + (j + 1), (j + 1) % DEPTH)
                    add(first + j, j, base[j])

            def early_end(k):
                dve.wait_ge(early_scaled, k + 1)
                nc.vector.tensor_tensor(early_sum, ps[:, EARLY_HI], early_sum, ALU.add
                                        ).then_inc(early_summed, 1)

            one_hots(0, 0)
            dve.wait_ge(zeroed, ROWS)
            nc.vector.engine_nop().then_inc(added, 2)
            nc.vector.engine_nop().then_inc(early_summed, 1)
            nc.vector.engine_nop().then_inc(early_free, 1)
            nc.vector.engine_nop().then_inc(y_ready, 2)
            build(group_pair, early_end=early_end, eng=dve)

            dve.wait_ge(added, GROUPS + 2)
            dve.wait_ge(early_stored, 16 * EARLY)
            nc.vector.memset(table1[:, BLOCKS - 1], 0.0)
            nc.vector.memset(bias_rows_all, 0.0).then_inc(bias_zero, 1)
            dve.wait_ge(bias_zero, 1)
            nc.vector.memset(bias_rows[0:1, :], 1.0).then_inc(work_zeroed, 1)
            dve.wait_ge(work_zeroed, 1)

            def peak(which, half, slot):
                return column(3 + which * CHUNKS + half * 2 + slot)

            for layer in range(3):
                def lead(half, slot, nodes, layer=layer):
                    q = position(layer, half, slot)
                    if layer == 0:
                        dve.wait_ge(deg_done, q + 1)
                        free(dve, rdeg_stored, q * 16)
                        free(dve, mean_ready, q)
                        nc.vector.tensor_reduce(peaks[:, peak(0, half, slot)],
                                                ps[:, DEG, 0:nodes], AX.X, ALU.max)
                        nc.vector.tensor_scalar(rdeg[:, 0:nodes], ps[:, DEG, 0:nodes], 1.0, None,
                                                ALU.max).then_inc(rdeg_step, 1)
                        free(dve, dense_done, q)
                        nc.vector.tensor_scalar(bias_rows[32:33, 0:nodes],
                                                ps[32:33, DEG, 0:nodes], 1.0, None, ALU.min
                                                ).then_inc(rdeg_step, 1)
                        dve.wait_ge(rdeg_step, q * 2 + 2)
                        nc.vector.reciprocal(rdeg[:, 0:nodes], rdeg[:, 0:nodes]
                                             ).then_inc(rdeg_ready, 1)
                    if layer or 2 * half + slot >= EARLY:
                        a = aggregated(layer, half, slot)
                        dve.wait_ge(lo_scaled, a + 1)
                        nc.vector.tensor_tensor(mean_T[:, slot, 0:nodes],
                                                ps[:, 2 * slot, 0:nodes],
                                                mean_T[:, slot, 0:nodes], ALU.add
                                                ).then_inc(summed, 1)
                        dve.wait_ge(summed, a + 1)
                    else:
                        dve.wait_ge(sum_loaded[slot], 16 * half + 16)
                    if layer == 0:
                        dve.wait_ge(rdeg_ready, q + 1)
                    else:
                        dve.wait_ge(rdeg_loaded, (q - (CHUNKS - 1)) * 16)
                    nc.vector.tensor_tensor(mean_T[:, slot, 0:nodes], mean_T[:, slot, 0:nodes],
                                            rdeg[:, 0:nodes], ALU.mult
                                            ).then_inc(mean_ready, 1)

                def post(half, slot, nodes, layer=layer):
                    q = position(layer, half, slot)
                    size = min(P, nodes)
                    count = 1 if nodes == LAST else SUB
                    mine = own[:, slot]
                    scratch = mean_T[:, slot].rearrange("p (t d) -> p t d", t=SUB)
                    dve.wait_ge(dense_done, q + 1)
                    if layer == 1:
                        dve.wait_ge(sigmoid_done, half * 2 + (slot + 1))
                        nc.vector.tensor_tensor(rows(mine, nodes),
                                                dense_rows(DENSE + slot, nodes),
                                                rows(scratch, nodes), ALU.mult
                                                ).then_inc(rows_ready, 1)
                    else:
                        before_it = mine if layer == 0 else residual
                        if layer == 2:
                            dve.wait_ge(residual_loaded, (half * 2 + (slot + 1)) * 16)
                        nc.vector.tensor_tensor(rows(mine, nodes),
                                                dense_rows(DENSE + slot, nodes),
                                                rows(before_it, nodes), ALU.add
                                                ).then_inc(y_ready, 1)
                        dve.wait_ge(y_ready, q + 3)
                        step = ln_steps(layer, half, slot)
                        for t in range(count):
                            last = nc.vector.bn_stats(stats[0:size, t], mine[0:size, t])
                        last.then_inc(ln_step, 1)
                        dve.wait_ge(ln_step, step + 1)
                        free(dve, rows_ready, q)
                        dve.sem_inc(waited, 1)
                        for t in range(count):
                            last = nc.vector.bn_aggr(moments[0:size, t], stats[0:size, t])
                        last.then_inc(ln_step, 1)
                        dve.wait_ge(std_ready, ln_chunks(layer, half, slot) + 1)
                        nc.vector.reciprocal(std[0:size, 0:count], std[0:size, 0:count]
                                             ).then_inc(ln_step, 1)
                        dve.wait_ge(ln_step, step + 3)
                        for t in range(count):
                            last = nc.vector.tensor_scalar(
                                mine[0:size, t], mine[0:size, t], moments[0:size, t, 0:1],
                                std[0:size, t:t + 1], ALU.subtract, ALU.mult)
                        last.then_inc(rows_ready, 1)
                    if layer < 2:
                        dve.wait_ge(rows_ready, q + 1)
                        if layer == 1:
                            values = mine[0:size, 0:count]
                            nc.vector.tensor_reduce(peaks[0:size, peak(1, half, slot)], values,
                                                    AX.XY, ALU.max, apply_absolute_value=True
                                                    ).then_inc(y_ready, 1)
                        dve.wait_ge(hi_ready, q + 1)
                        nc.vector.tensor_tensor(
                            rows(scratch, nodes), rows(mine, nodes),
                            table_rows((table1, table0)[layer], half, slot, nodes, 0),
                            ALU.subtract).then_inc(rest_ready, 1)

                if layer == 2:
                    dve.wait_ge(y_ready, 2 * CHUNKS + 2)
                    nc.vector.tensor_tensor(over, peaks, limits, ALU.is_gt).then_inc(over_step, 1)
                    dve.wait_ge(over_step, 1)
                    nc.vector.tensor_reduce(any_over, over, AX.X, ALU.max).then_inc(any_ready, 1)
                    dve.wait_ge(over_counted, 1)
                    nc.vector.tensor_copy(flag[0:1, :], ps[0:1, DEG, 0:1]).then_inc(flag_ready, 1)
                lead_and_post(dve, layer, lead, post)
            general_vector(dve)


def kernel(**inputs):
    import concourse.bacc as bacc
    from concourse.bass_utils import run_bass_kernel_spmd

    arrays = {}

    def lay(name, array):
        arrays[name] = np.ascontiguousarray(array)

    def edges(a, pad):
        a = np.asarray(a)
        padded = np.full(TILES * P, pad, a.dtype)
        padded[0:E] = a
        return padded.reshape(TILES, P).T

    dst = edges(inputs["dst"], NO_NODE)
    lay("x", inputs["x"])
    lay("src_t", edges(inputs["src"], 0))
    lay("dst_t", dst)
    lay("type_t", edges(inputs["edge_type_64"], 0))
    lay("first_dst", dst[0, ::GROUP])
    lay("rel_emb", inputs["L0_gnn_rel_emb"])
    for name, given in (("w_msg", "L0_gnn_W_msg"), ("w_self", "L0_gnn_W_self"),
                        ("w1_l", "L1_gnn_W1_l"), ("w1_r", "L1_gnn_W1_r"),
                        ("w2_l", "L1_gnn_W2_l"), ("w2_r", "L1_gnn_W2_r")):
        lay(name, np.asarray(inputs[given]).T)
    for name, given in (("b_self", "L0_gnn_b_self"), ("b_msg", "L0_gnn_b_msg"),
                        ("b1", "L1_gnn_b1"), ("b2", "L1_gnn_b2")):
        lay(name, np.asarray(inputs[given]).reshape(1, D))

    nc = bacc.Bacc("TRN2", target_bir_lowering=False, num_devices=1)
    args = {name: nc.dram_tensor(name, a.shape, mybir.dt.from_np(a.dtype),
                                 kind="ExternalInput").ap() for name, a in arrays.items()}
    for name, shape in (("x1_dram", (N, D)), ("h_dram", (N, D)), ("rdeg_dram", (P, N)),
                        ("sum_dram", (P, EARLY * CHUNK))):
        args[name] = nc.dram_tensor(name, shape, F32, kind="Internal").ap()
    args["out"] = nc.dram_tensor("out", (N, D), F32, kind="ExternalOutput").ap()
    gnn_program(nc, **args)
    return run_bass_kernel_spmd(nc, [arrays], core_ids=[0]).results[0]["out"]
```

```python
from contextlib import ExitStack

import numpy as np

import concourse.bass as bass
from concourse import mybir

ALU = mybir.AluOpType
ACT = mybir.ActivationFunctionType
AX = mybir.AxisListType
F32 = mybir.dt.float32
F16 = mybir.dt.float16
I32 = mybir.dt.int32
U32 = mybir.dt.uint32
DVE = mybir.EngineType.DVE

P = 128
N = 3125
D = 128
E = 53125
RELATIONS = 64
TILES = 416
FULL_TILES = E // P
GROUP = 2
GROUPS = TILES // GROUP
DEPTH = 2
WINDOW = 24
BLOCKS = (N + P - 1) // P
ROWS = BLOCKS + 1
HALF = ROWS // 2
COMBINED = BLOCKS * WINDOW
WIDTH = 3152
QUARTER = WIDTH // 4
CHUNK = 512
CHUNKS = (N + CHUNK - 1) // CHUNK
LAST = N - CHUNK * (CHUNKS - 1)
SUB = CHUNK // P
SPLIT = 2048.0
EARLY = 5
PERIOD = 34
LEAD = 40
UNROLL = 8
EARLY_GROUPS = ROWS - 2
MOST_EDGES = 2048.0
MOST_VALUE = 60000.0
PEAKS = 3 + 2 * CHUNKS
EPS = 1e-5
NO_NODE = 4096
WEIGHTS = ("w_msg", "w_self", "w1_l", "w1_r", "w2_l", "w2_r")
assert LEAD % UNROLL == EARLY_GROUPS % UNROLL == GROUPS % UNROLL == ROWS % 2 == 0
assert LEAD + PERIOD * (EARLY - 1) + EARLY_GROUPS + DEPTH < GROUPS
assert WIDTH % 8 == 0 and WIDTH >= N - 1 + WINDOW and HALF * WINDOW <= 512 and LAST <= P and CHUNKS == 7


def gnn_program(nc, x, src_t, dst_t, type_t, first_dst, rel_emb, w_msg, w_self, w1_l, w1_r,
                w2_l, w2_r, b_self, b_msg, b1, b2, x1_dram, h_dram, rdeg_dram, sum_dram, out):
    with ExitStack() as ctx:
        def sb(name, shape, dtype=F32):
            return ctx.enter_context(nc.sbuf_tensor(name, shape, dtype))

        def sem(name):
            return ctx.enter_context(nc.semaphore(name))

        A = sb("counts", [P, ROWS, WIDTH], F16)
        table0 = sb("table0", [P, ROWS, 2, D], F16)
        weights = sb("weights", [P, 6, D])
        bias = sb("bias", [33, 3, D])
        ident = sb("ident", [P, P])
        ones_h = sb("ones_h", [P, P], F16)
        eps_col = sb("eps_col", [P, 1])

        WORK = 7480
        work = sb("work", [P, WORK])

        def view(at, count, dtype=F32):
            words = count * (2 if dtype == F16 else 4) // 4
            assert at + words <= WORK, (at, words)
            piece = work[:, at:at + words]
            return (piece if dtype == F32 else piece.bitcast(dtype)), at + words

        at = 0
        iota_c, at = view(at, COMBINED, F16)
        iota_p, at = view(at, P, F16)
        PADDED = TILES + 2 * GROUP
        flat, at = view(at, PADDED * 4)
        edge_f = flat.rearrange("p (t k) -> p t k", k=4)
        combined_f, offset_f, type_f = (edge_f[:, 0:TILES, k] for k in (0, 2, 3))
        low_f = edge_f[:, :, 1]
        flat, at = view(at, DEPTH * GROUP)
        fetched = flat.rearrange("p (g t) -> p g t", g=DEPTH)
        base_i, at = view(at, GROUPS, I32)
        delta_i, at = view(at, GROUPS, I32)
        flat, at = view(at, DEPTH * ROWS)
        carry = flat.rearrange("p (s a b w) -> p s a b w", s=DEPTH, a=2, w=1)
        M_AT = at
        hot, at = view(at, DEPTH * GROUP * COMBINED, F16)
        M = hot.rearrange("p (g t c) -> p g t c", g=DEPTH, t=GROUP)
        hot, at = view(at, DEPTH * GROUP * P, F16)
        LOW = hot.rearrange("p (g t c) -> p g t c", g=DEPTH, t=GROUP)
        hot, at = view(at, DEPTH * GROUP * P, F16)
        TYPE = hot.rearrange("p (g t c) -> p g t c", g=DEPTH, t=GROUP)
        hot, at = view(at, DEPTH * GROUP * WINDOW, F16)
        WIN = hot.rearrange("p (g t c) -> p g t c", g=DEPTH, t=GROUP)
        early_sum, at = view(at, CHUNK)
        build_end = at

        stage = A[:].rearrange("p b w -> p (b w)").bitcast(F32).rearrange(
            "p (b w) -> p b w", b=ROWS)
        at = WIDTH // 2 - D
        stage_x = stage[:, :, at:at + D]

        def staged(block, count):
            return stage[:, block, at - TILES:at - TILES + count].bitcast(I32)

        src_i, dst_i, type_i, block_i, low_i = (staged(block, TILES) for block in range(5))
        first_i = staged(5, GROUPS)
        floors = stage[:, 6, at - TILES:at - TILES + GROUPS]

        off_middle, late = (work[:, M_AT + k * (TILES + GROUPS):M_AT + (k + 1) * (TILES + GROUPS)
                                 ] for k in range(2))
        late = late[:, 0:TILES]
        assert (TILES + GROUPS) * 2 <= DEPTH * GROUP * (COMBINED + P) // 2

        at = 0
        second, at = view(at, BLOCKS * 2 * D, F16)
        table1 = second.rearrange("p (b s d) -> p b s d", b=BLOCKS, s=2)
        flat, at = view(at, CHUNK)
        residual = flat.rearrange("p (t d) -> p t d", t=SUB)
        own_T, at = view(at, CHUNK)
        rdeg, at = view(at, CHUNK)
        flat, at = view(at, SUB * 6)
        stats = flat.rearrange("p (t k) -> p t k", t=SUB)
        flat, at = view(at, SUB * 2)
        moments = flat.rearrange("p (t k) -> p t k", t=SUB)
        std, at = view(at, SUB)
        bias_rows_all, at = view(at, CHUNK)
        bias_rows = bias_rows_all[0:33, :]
        assert at >= build_end
        flat, at = view(at, 2 * CHUNK)
        own = flat.rearrange("p (s t d) -> p s t d", s=2, t=SUB)
        zeros = flat[:, 0:QUARTER // 2]
        flat, at = view(at, 2 * CHUNK)
        mean_T = flat.rearrange("p (s n) -> p s n", s=2)
        peaks, at = view(at, PEAKS)
        limits, at = view(at, PEAKS)
        over, at = view(at, PEAKS)
        any_over, at = view(at, 1)
        ones_col, at = view(at, 1)
        flag, at = view(at, 1, I32)
        spare, at = view(at, 1)

        ps = ctx.enter_context(nc.psum_tensor("ps", [P, 8, 512], F32))
        DEG, DENSE, TURN = 4, 5, 7
        EARLY_HI, EARLY_LO = 4, 5

        edges_in = sem("edges_in")
        x_in = [sem(f"x_in{k}") for k in range(2)]
        weights_in = sem("weights_in")
        constants = sem("constants")
        pads_zero = sem("pads_zero")
        edge_step = sem("edge_step")
        scalars_ready = sem("scalars_ready")
        x_hi = sem("x_hi")
        x_rest = sem("x_rest")
        x_lo = sem("x_lo")
        v_hot = sem("v_hot")
        p_hot = sem("p_hot")
        p_fetched = sem("p_fetched")
        counted = sem("counted")
        joined = sem("joined")
        carried = sem("carried")
        zeros_ready = sem("zeros_ready")
        first_zeroed = sem("first_zeroed")
        rest_zeroed = sem("rest_zeroed")
        copied = sem("copied")
        bias_zero = sem("bias_zero")
        early_done = sem("early_done")
        early_scaled = sem("early_scaled")
        early_summed = sem("early_summed")
        early_stored = sem("early_stored")
        early_free = sem("early_free")
        sum_loaded = [sem(f"sum_loaded{k}") for k in range(2)]
        waited = sem("waited")
        over_step = sem("over_step")
        any_ready = sem("any_ready")
        over_counted = sem("over_counted")
        flag_ready = sem("flag_ready")
        check_step = sem("check_step")
        edges_checked = sem("edges_checked")
        work_zeroed = sem("work_zeroed")
        agg_done = sem("agg_done")
        deg_done = sem("deg_done")
        turned = sem("turned")
        dense_done = sem("dense_done")
        lo_scaled = sem("lo_scaled")
        own_T_ready = sem("own_T_ready")
        sigmoid_done = sem("sigmoid_done")
        std_ready = sem("std_ready")
        hi_ready = sem("hi_ready")
        lo_ready = sem("lo_ready")
        rdeg_step = sem("rdeg_step")
        rdeg_ready = sem("rdeg_ready")
        summed = sem("summed")
        mean_ready = sem("mean_ready")
        y_ready = sem("y_ready")
        ln_step = sem("ln_step")
        rows_ready = sem("rows_ready")
        rest_ready = sem("rest_ready")
        own_loaded = [sem(f"own_loaded{k}") for k in range(2)]
        residual_loaded = sem("residual_loaded")
        rdeg_loaded = sem("rdeg_loaded")
        rdeg_stored = sem("rdeg_stored")
        rows_stored = [sem(f"rows_stored{k}") for k in range(2)]

        IN_SLOT = [(CHUNKS + 1) // 2, CHUNKS // 2]

        def before(layer, half, slot):
            return layer * IN_SLOT[slot] + half

        def position(layer, half, slot):
            return layer * CHUNKS + half * 2 + slot

        def free(eng, semaphore, value):
            if not isinstance(value, int) or value > 0:
                eng.wait_ge(semaphore, value)

        def counts_of(slot):
            return ps[:, 2 * slot:2 * slot + 2, 0:HALF * WINDOW].rearrange(
                "p a (b w) -> p a b w", w=WINDOW)

        def aggregated(layer, half, slot):
            return position(layer, half, slot) - EARLY

        def lead_and_post(eng, layer, lead, post, turn=None):
            turn = turn or (lambda *chunk: None)
            last = CHUNKS // 2
            lead(0, 0, CHUNK)
            turn(0, 0, CHUNK)

            def pair(half):
                for now, then in (((half, 1, CHUNK), (half, 0, CHUNK)),
                                  ((half + 1, 0, CHUNK), (half, 1, CHUNK))):
                    lead(*now)
                    post(*then)
                    turn(*now)

            pair(0)
            if layer == 0:
                for half in range(1, last - 1):
                    pair(half)
            else:
                with eng.Fori(1, last - 1) as half:
                    pair(half)
            lead(last - 1, 1, CHUNK)
            post(last - 1, 0, CHUNK)
            turn(last - 1, 1, CHUNK)
            lead(last, 0, LAST)
            post(last - 1, 1, CHUNK)
            turn(last, 0, LAST)
            post(last, 0, LAST)

        def nodes_at(half, slot, nodes):
            start = half * (2 * CHUNK) + slot * CHUNK
            return slice(start, start + nodes) if isinstance(start, int) else bass.ds(start, nodes)

        def dram_rows(dram, half, slot, nodes):
            rows = dram[nodes_at(half, slot, nodes), :]
            return rows if nodes == LAST else rows.rearrange("(t p) d -> p t d", p=P)

        def rows(buffer, nodes):
            return buffer[0:LAST, 0, :] if nodes == LAST else buffer

        def table_rows(table, half, slot, nodes, part):
            if nodes == LAST:
                return table[0:LAST, BLOCKS - 1, part, :]
            first = half * (2 * SUB) + slot * SUB
            span = slice(first, first + SUB) if isinstance(first, int) else bass.ds(first, SUB)
            return table[:, span, part, :]

        def dense_rows(bank, nodes):
            if nodes == LAST:
                return ps[0:LAST, bank, 0:D]
            return ps[:, bank, :].rearrange("p (t d) -> p t d", t=SUB)

        def column(tile):
            return slice(tile, tile + 1) if isinstance(tile, int) else bass.ds(tile, 1)

        def columns(tile):
            return slice(tile, tile + GROUP) if isinstance(tile, int) else bass.ds(tile, GROUP)

        def ln_chunks(layer, half, slot):
            return (0 if layer == 0 else CHUNKS) + half * 2 + slot

        def ln_steps(layer, half, slot):
            return ln_chunks(layer, half, slot) * 3

        free_words = A[:].rearrange("p b w -> p (b w)").bitcast(F32)

        def placed(at, count, dtype=F32):
            piece = free_words[:, at:at + count]
            return (piece if dtype == F32 else piece.bitcast(dtype)), at + count

        g_iota, at = placed(0, N)
        g_hot, at = placed(at, N)
        g_mean_T, at = placed(at, N)
        g_rdeg, at = placed(at, N)
        g_rows_of_bias, at = placed(at, N)
        g_bias_rows = g_rows_of_bias[0:33]
        g_src, at = placed(at, TILES, I32)
        g_dst, at = placed(at, TILES, I32)
        g_type, at = placed(at, TILES, I32)
        g_dst_f, at = placed(at, TILES)
        g_index, at = placed(at, 2, I32)
        g_ones, at = placed(at, P)
        g_source, at = placed(at, D)
        g_relation, at = placed(at, D)
        g_own, at = placed(at, D)
        g_residual, at = placed(at, D)
        g_own_T, at = placed(at, P)
        g_mean_tile, at = placed(at, P)
        g_bias_tile, at = placed(at, P)
        g_sigmoid, at = placed(at, D)
        g_new, at = placed(at, D)
        g_stats, at = placed(at, 6)
        g_moments, at = placed(at, 2)
        g_std, at = placed(at, 1)
        G_TURN, G_DENSE = slice(0, P), slice(P, P + D)

        gs_edges = sem("general_edges")
        gs_setup = sem("general_setup")
        gs_lists = sem("general_lists")
        gs_index = sem("general_index")
        gs_source = sem("general_source")
        gs_relation = sem("general_relation")
        gs_message = sem("general_message")
        gs_hot = sem("general_hot")
        gs_counted = sem("general_counted")
        gs_pass = sem("general_pass")
        gs_own = sem("general_own")
        gs_turned = sem("general_turned")
        gs_own_T = sem("general_own_T")
        gs_dense = sem("general_dense")
        gs_sigmoid = sem("general_sigmoid")
        gs_std = sem("general_std")
        gs_step = sem("general_step")
        gs_row = sem("general_row")
        gs_stored = sem("general_stored")

        def hold(eng, semaphore, value):
            if not isinstance(value, int) or value > 0:
                eng.wait_ge(semaphore, value)
                eng.sem_inc(waited, 1)

        def if_over(eng, engine_type, general):
            eng.wait_ge(flag_ready, 1)
            found = nc.values_load_multi_w_load_instructions(
                flag[0:1, 0:1], engines=[engine_type], min_val=0, max_val=P,
                skip_runtime_bounds_check_because="it counts partitions")[1][0]
            with eng.If(found != 0):
                for slot in range(2):
                    eng.wait_ge(rows_stored[slot], 16 * before(3, 0, slot))
                eng.sem_inc(waited, 1)
                general()

        def edge_tiles(eng, step):
            step(0, True)
            with eng.Fori(1, TILES) as tile:
                step(tile, False)

        def node_tiles(eng, step):
            step(0, P)
            with eng.Fori(1, BLOCKS - 1) as tile:
                step(tile, P)
            step(BLOCKS - 1, N - P * (BLOCKS - 1))

        def node_span(tile, size):
            return slice(tile * P, tile * P + size) if isinstance(tile, int) else bass.ds(
                tile * P, size)

        def general_sync(sp):
            def general():
                for to, given in ((g_src, src_t), (g_dst, dst_t), (g_type, type_t)):
                    sp.dma_start(to, given).then_inc(gs_edges, 16)
                for layer, (source, sink) in enumerate(((x, x1_dram), (x1_dram, h_dram),
                                                        (h_dram, out))):
                    def step(tile, size, layer=layer, source=source, sink=sink):
                        q = layer * BLOCKS + tile
                        span = node_span(tile, size)
                        hold(sp, gs_stored, q * 16)
                        sp.dma_start(g_own[0:size], source[span, :]).then_inc(gs_own, 16)
                        sp.dma_start(g_residual[0:size], (x1_dram if layer == 2 else source)
                                     [span, :]).then_inc(gs_own, 16)
                        hold(sp, gs_row, q + 1)
                        sp.dma_start(sink[span, :], g_new[0:size]).then_inc(gs_stored, 16)

                    node_tiles(sp, step)
                sp.wait_ge(gs_stored, 16 * 3 * BLOCKS)

            if_over(sp, mybir.EngineType.SP, general)

        def general_gpsimd(pool):
            def general():
                nc.gpsimd.iota(g_iota, [[1, N]], base=0, channel_multiplier=0,
                               allow_small_or_imprecise_dtypes=True).then_inc(gs_setup, 1)
                nc.gpsimd.memset(g_ones, 1.0).then_inc(gs_setup, 1)
                nc.gpsimd.memset(g_rows_of_bias, 0.0).then_inc(gs_setup, 1)
                pool.wait_ge(gs_setup, 3)
                nc.gpsimd.memset(g_rows_of_bias[0:1], 1.0).then_inc(gs_setup, 1)
                pool.wait_ge(gs_lists, 1)
                for layer, source in enumerate((x, x1_dram, h_dram)):
                    hold(pool, gs_stored, 16 * BLOCKS * layer)

                    def step(tile, _, layer=layer, source=source):
                        n = layer * TILES + tile
                        hold(pool, gs_counted, n + TILES)
                        nc.gpsimd.tensor_copy(g_index[:, 0:1], g_src[:, column(tile)]
                                              ).then_inc(gs_index, 1)
                        nc.gpsimd.tensor_copy(g_index[:, 1:2], g_type[:, column(tile)]
                                              ).then_inc(gs_index, 1)
                        hold(pool, gs_index, 2 * n + 2)
                        nc.gpsimd.indirect_dma_start(
                            g_source, None, source,
                            bass.IndirectOffsetOnAxis(ap=g_index[:, 0:1], axis=0)
                        ).then_inc(gs_source, 16)
                        if layer == 0:
                            nc.gpsimd.indirect_dma_start(
                                g_relation, None, rel_emb,
                                bass.IndirectOffsetOnAxis(ap=g_index[:, 1:2], axis=0)
                            ).then_inc(gs_relation, 16)

                    edge_tiles(pool, step)

            if_over(pool, mybir.EngineType.Pool, general)

        def general_scalar(act):
            def general():
                for layer in range(3):
                    act.wait_ge(gs_pass, layer + 2)

                    def step(tile, size, layer=layer):
                        q = layer * BLOCKS + tile
                        span = node_span(tile, size)
                        hold(act, gs_turned, q + 1)
                        nc.scalar.copy(g_mean_tile[:, 0:size], g_mean_T[:, span])
                        nc.scalar.copy(g_bias_tile[0:33, 0:size], g_bias_rows[:, span])
                        nc.scalar.copy(g_own_T[:, 0:size], ps[:, 7, 0:size]
                                       ).then_inc(gs_own_T, 1)
                        if layer == 1:
                            hold(act, gs_dense, q + 1)
                            nc.scalar.activation(g_sigmoid[0:size], ps[0:size, 7, G_DENSE],
                                                 ACT.Sigmoid).then_inc(gs_sigmoid, 1)
                        else:
                            normalised = (0 if layer == 0 else BLOCKS) + tile
                            hold(act, gs_step, normalised * 4 + 3)
                            nc.scalar.activation(g_std[0:size], g_moments[0:size, 1:2],
                                                 ACT.Sqrt, bias=eps_col[0:size]
                                                 ).then_inc(gs_std, 1)

                    node_tiles(act, step)

            if_over(act, mybir.EngineType.Activation, general)

        def general_tensor(pe):
            def general():
                pe.wait_ge(gs_setup, 4)
                for k in range(4):
                    hold(pe, gs_pass, k)
                    hold(pe, gs_row, BLOCKS * (k - 1))

                    def step(tile, first, k=k):
                        hold(pe, gs_hot, k * TILES + tile + 1)
                        if k == 1:
                            hold(pe, gs_message, tile + 1)
                        elif k > 1:
                            hold(pe, gs_source, ((k - 1) * TILES + tile) * 16 + 16)
                        for c in range(CHUNKS):
                            nodes = CHUNK if c < CHUNKS - 1 else LAST
                            last = nc.tensor.matmul(
                                ps[:, c, 0:nodes], g_source if k else g_ones,
                                g_hot[:, c * CHUNK:c * CHUNK + nodes],
                                start=first, stop=not first, skip_group_check=True)
                        last.then_inc(gs_counted, 1)

                    edge_tiles(pe, step)
                    if k == 0:
                        continue
                    hold(pe, gs_pass, k + 1)

                    def dense(tile, size, layer=k - 1):
                        q = layer * BLOCKS + tile
                        hold(pe, gs_own, q * 32 + 32)
                        nc.tensor.transpose(ps[:, 7, 0:size], g_own[0:size],
                                            ident[0:size, 0:size]).then_inc(gs_turned, 1)
                        hold(pe, gs_own_T, q + 1)
                        to = ps[0:size, 7, G_DENSE]
                        keep = 33 if layer == 0 else 1
                        nc.tensor.matmul(to, g_mean_tile[:, 0:size],
                                         weights[:, 2 * layer, :], start=True, stop=False)
                        nc.tensor.matmul(to, g_own_T[:, 0:size], weights[:, 2 * layer + 1, :],
                                         start=False, stop=False)
                        nc.tensor.matmul(to, g_bias_tile[0:keep, 0:size],
                                         bias[0:keep, layer, :],
                                         start=False, stop=True).then_inc(gs_dense, 1)

                    node_tiles(pe, dense)

            if_over(pe, mybir.EngineType.PE, general)

        def general_vector(dve):
            def general():
                dve.wait_ge(gs_edges, 48)
                nc.vector.tensor_copy(g_dst_f, g_dst)
                nc.vector.tensor_scalar(g_type, g_type, 0, RELATIONS - 1, ALU.max, ALU.min
                                        ).then_inc(gs_lists, 1)
                dve.wait_ge(gs_lists, 1)
                dve.wait_ge(gs_setup, 4)
                sums = ps[:].rearrange("p b c -> p (b c)")[:, 0:N]
                for k in range(4):
                    def step(tile, _, k=k):
                        n = k * TILES + tile
                        hold(dve, gs_counted, n)
                        nc.vector.tensor_scalar(g_hot, g_iota, g_dst_f[:, column(tile)], None,
                                                ALU.is_equal).then_inc(gs_hot, 1)
                        if k == 1:
                            hold(dve, gs_source, tile * 16 + 16)
                            hold(dve, gs_relation, tile * 16 + 16)
                            nc.vector.tensor_tensor(g_source, g_source, g_relation, ALU.add
                                                    ).then_inc(gs_message, 1)

                    edge_tiles(dve, step)
                    hold(dve, gs_counted, (k + 1) * TILES)
                    if k == 0:
                        nc.vector.tensor_scalar(g_rdeg, sums, 1.0, None, ALU.max)
                        nc.vector.tensor_scalar(g_bias_rows[32:33], sums[32:33], 1.0, None,
                                                ALU.min).then_inc(gs_lists, 1)
                        dve.wait_ge(gs_lists, 2)
                        nc.vector.reciprocal(g_rdeg, g_rdeg).then_inc(gs_pass, 1)
                        dve.wait_ge(gs_pass, 1)
                        continue
                    nc.vector.tensor_tensor(g_mean_T, sums, g_rdeg, ALU.mult
                                            ).then_inc(gs_pass, 1)

                    def rows_of(tile, size, layer=k - 1):
                        q = layer * BLOCKS + tile
                        y = g_new[0:size]
                        products = ps[0:size, 7, G_DENSE]
                        if layer == 1:
                            hold(dve, gs_sigmoid, tile + 1)
                            nc.vector.tensor_tensor(y, products, g_sigmoid[0:size], ALU.mult
                                                    ).then_inc(gs_row, 1)
                            return
                        done = ((0 if layer == 0 else BLOCKS) + tile) * 4
                        hold(dve, gs_dense, q + 1)
                        nc.vector.tensor_tensor(y, products, g_residual[0:size], ALU.add
                                                ).then_inc(gs_step, 1)
                        hold(dve, gs_step, done + 1)
                        nc.vector.bn_stats(g_stats[0:size], y).then_inc(gs_step, 1)
                        hold(dve, gs_step, done + 2)
                        nc.vector.bn_aggr(g_moments[0:size], g_stats[0:size]
                                          ).then_inc(gs_step, 1)
                        hold(dve, gs_std, (0 if layer == 0 else BLOCKS) + tile + 1)
                        nc.vector.reciprocal(g_std[0:size], g_std[0:size]
                                             ).then_inc(gs_step, 1)
                        hold(dve, gs_step, done + 4)
                        nc.vector.tensor_scalar(y, y, g_moments[0:size, 0:1], g_std[0:size],
                                                ALU.subtract, ALU.mult).then_inc(gs_row, 1)

                    node_tiles(dve, rows_of)

            if_over(dve, mybir.EngineType.DVE, general)

        def zero_first(memset, first_block, last_block):
            memset(A[:, first_block:last_block, 0:QUARTER].bitcast(U32), 0
                   ).then_inc(first_zeroed, 1)

        def build(eng, step, early_start=None, early_block=None, early_end=None,
                  after_lead=None):
            with eng.Fori(0, LEAD // UNROLL) as i:
                step(i * UNROLL, UNROLL)
            if after_lead:
                after_lead()

            def period(k, length):
                if early_start:
                    early_start(k)
                first = k * PERIOD + LEAD
                with eng.Fori(0, EARLY_GROUPS // UNROLL) as i:
                    step(first + i * UNROLL, UNROLL,
                         early_block and (lambda j: early_block(k, i * UNROLL + (1 + j))))
                step(first + EARLY_GROUPS, DEPTH)
                if early_end:
                    early_end(k)
                step(first + (EARLY_GROUPS + DEPTH), length - EARLY_GROUPS - DEPTH)

            with eng.Fori(0, EARLY - 1) as k:
                period(k, PERIOD)
            period(EARLY - 1, GROUPS - LEAD - PERIOD * (EARLY - 1))

        block = ctx.enter_context(nc.Block())

        @block.sync
        def _(sp):
            cut = HALF * P
            full = (BLOCKS - 1) * P
            sp.dma_start(stage_x[:, 0:HALF, :], x[0:cut, :].rearrange("(b p) d -> p b d", p=P)
                         ).then_inc(x_in[0], 16)
            sp.dma_start(stage_x[:, HALF:BLOCKS - 1, :],
                         x[cut:full, :].rearrange("(b p) d -> p b d", p=P)
                         ).then_inc(x_in[1], 16)
            sp.wait_ge(pads_zero, 1)
            sp.dma_start(stage_x[0:N - full, BLOCKS - 1, :], x[full:N, :]).then_inc(x_in[1], 16)
            sp.dma_start(stage_x[0:RELATIONS, BLOCKS, :], rel_emb).then_inc(x_in[1], 16)
            sp.wait_ge(constants, 1)
            for k, w in enumerate((w_msg, w_self, w1_l, w1_r, w2_l, w2_r)):
                sp.dma_start(weights[:, k, :], w).then_inc(weights_in, 16)
            for row, k, b in ((0, 0, b_self), (32, 0, b_msg), (0, 1, b1), (0, 2, b2)):
                sp.dma_start(bias[row:row + 1, k, :], b).then_inc(weights_in, 16)

            for quarter in range(1, 4):
                if quarter == 1:
                    sp.wait_ge(zeros_ready, 1)
                elif quarter == 2:
                    sp.wait_ge(scalars_ready, 1)
                else:
                    sp.wait_ge(x_lo, 2)
                sp.dma_start(
                    A[:, :, quarter * QUARTER:(quarter + 1) * QUARTER].bitcast(F32),
                    zeros.unsqueeze(1).to_broadcast([P, ROWS, QUARTER // 2])
                ).then_inc(rest_zeroed, 16)

            with sp.Fori(0, EARLY) as k:
                sp.wait_ge(early_summed, k + 2)
                sp.sem_inc(waited, 1)
                sp.dma_start(sum_dram[:, bass.ds(k * CHUNK, CHUNK)], early_sum
                             ).then_inc(early_stored, 16)
                sp.wait_ge(early_stored, k * 16 + 16)
                sp.sem_inc(early_free, 1)

            for layer, (source, sink) in enumerate(((x, x1_dram), (x1_dram, h_dram),
                                                    (h_dram, out))):
                def load(half, slot, nodes, layer=layer, source=source):
                    free(sp, rows_stored[slot], before(layer, half, slot) * 16)
                    sp.sem_inc(waited, 1)
                    q = position(layer, half, slot)
                    first = isinstance(half, int) and half == 0
                    if layer < 2:
                        used = q if layer and slot == 0 and first else q - 1
                        free(sp, hi_ready, used)
                        free(sp, rest_ready, used)
                    elif first:
                        sp.wait_ge(hi_ready, 2 * CHUNKS)
                        sp.wait_ge(rest_ready, 2 * CHUNKS)
                    sp.dma_start(rows(own[:, slot], nodes), dram_rows(source, half, slot, nodes)
                                 ).then_inc(own_loaded[slot], 16)

                def store(half, slot, nodes, layer=layer, sink=sink):
                    sp.wait_ge(rows_ready, position(layer, half, slot) + 1)
                    sp.dma_start(dram_rows(sink, half, slot, nodes), rows(own[:, slot], nodes)
                                 ).then_inc(rows_stored[slot], 16)

                def load_residual(half, slot, nodes):
                    sp.dma_start(rows(residual, nodes), dram_rows(x1_dram, half, slot, nodes)
                                 ).then_inc(residual_loaded, 16)

                load(0, 0, CHUNK)
                load(0, 1, CHUNK)
                if layer == 2:
                    load_residual(0, 0, CHUNK)
                with sp.Fori(0, 2) as half:
                    for slot in range(2):
                        store(half, slot, CHUNK)
                        if layer == 2:
                            load_residual(*((half, 1) if slot == 0 else (half + 1, 0)), CHUNK)
                        load(half + 1, slot, CHUNK)
                store(2, 0, CHUNK)
                if layer == 2:
                    load_residual(2, 1, CHUNK)
                load(3, 0, LAST)
                store(2, 1, CHUNK)
                if layer == 2:
                    load_residual(3, 0, LAST)
                store(3, 0, LAST)
            for slot in range(2):
                sp.wait_ge(rows_stored[slot], 16 * before(3, 0, slot))
            general_sync(sp)

        @block.gpsimd
        def _(pool):
            nc.gpsimd.memset(bias[:], 0.0).then_inc(constants, 1)
            nc.gpsimd.iota(iota_c, [[1, COMBINED]], base=0, channel_multiplier=0,
                           allow_small_or_imprecise_dtypes=True).then_inc(constants, 1)
            nc.gpsimd.iota(iota_p, [[1, P]], base=0, channel_multiplier=0,
                           allow_small_or_imprecise_dtypes=True).then_inc(constants, 1)
            nc.gpsimd.memset(ones_h[:], 1.0).then_inc(constants, 1)
            nc.gpsimd.memset(eps_col[:], EPS).then_inc(constants, 1)
            nc.gpsimd.memset(ident[:], 0.0).then_inc(constants, 1)
            nc.gpsimd.memset(ones_col, 1.0).then_inc(constants, 1)
            pool.wait_ge(constants, 7)
            nc.gpsimd.affine_select(out=ident[:], in_=ident[:], compare_op=ALU.not_equal,
                                    fill=1.0, base=0, pattern=[[-1, P]],
                                    channel_multiplier=1).then_inc(constants, 1)
            zero_first(nc.gpsimd.memset, 0, 8)
            pool.wait_ge(scalars_ready, 1)

            def fetch(group, slot):
                nc.gpsimd.tensor_copy(fetched[:, slot], low_f[:, columns(group * GROUP)]
                                      ).then_inc(p_fetched, 1)

            def one_hots(group, slot):
                pool.wait_ge(p_fetched, group + 1)
                pool.wait_ge(p_hot, group + 1)
                fetch(group + 1, 1 - slot)
                for t in range(GROUP - slot):
                    last = nc.gpsimd.tensor_scalar(LOW[:, slot, t], iota_p,
                                                   fetched[:, slot, t:t + 1], None, ALU.is_equal)
                last.then_inc(p_hot, 1)

            pool.sem_inc(p_hot, 1)
            fetch(0, 0)
            with pool.Fori(0, GROUPS // UNROLL) as i:
                for j in range(UNROLL):
                    pool.wait_ge(counted, i * UNROLL + (j + 1))
                    one_hots(i * UNROLL + j, j % DEPTH)

            pool.wait_ge(early_stored, 16 * EARLY)

            def load_sum(chunk):
                half, slot = divmod(chunk, 2)
                free(pool, dense_done, chunk - 1)
                free(pool, lo_ready, chunk - 1)
                pool.dma_start(mean_T[:, slot], sum_dram[:, nodes_at(half, slot, CHUNK)]
                               ).then_inc(sum_loaded[slot], 16)

            load_sum(0)
            load_sum(1)
            for chunk in range(CHUNKS):
                nodes = CHUNK if chunk < CHUNKS - 1 else LAST
                pool.wait_ge(rdeg_ready, chunk + 1)
                pool.dma_start(rdeg_dram[:, nodes_at(chunk // 2, chunk % 2, nodes)],
                               rdeg[:, 0:nodes]).then_inc(rdeg_stored, 16)
                if 2 <= chunk + 1 < EARLY:
                    load_sum(chunk + 1)
            pool.wait_ge(rdeg_stored, 16 * CHUNKS)
            for layer in (1, 2):
                def load_rdeg(half, slot, nodes, layer=layer):
                    pool.wait_ge(mean_ready, position(layer, half, slot))
                    pool.dma_start(rdeg[:, 0:nodes], rdeg_dram[:, nodes_at(half, slot, nodes)]
                                   ).then_inc(rdeg_loaded, 16)

                with pool.Fori(0, 3) as half:
                    load_rdeg(half, 0, CHUNK)
                    load_rdeg(half, 1, CHUNK)
                load_rdeg(3, 0, LAST)
            general_gpsimd(pool)

        @block.scalar
        def _(act):
            for to, given in ((dst_i, dst_t), (src_i, src_t), (type_i, type_t)):
                act.dma_start(to, given).then_inc(edges_in, 16)
            act.dma_start(first_i, first_dst.partition_broadcast(P)).then_inc(edges_in, 16)
            zero_first(lambda out, _: nc.scalar.memzero(out), 8, 17)
            halves = [slice(k * HALF, (k + 1) * HALF) for k in range(2)]
            for k, half in enumerate(halves):
                act.wait_ge(x_in[k], (16, 48)[k])
                nc.scalar.activation(table0[:, half, 0, :], stage_x[:, half], ACT.Copy
                                     ).then_inc(x_hi, 1)
            for k, half in enumerate(halves):
                act.wait_ge(x_rest, k + 1)
                nc.scalar.activation(table0[:, half, 1, :], stage_x[:, half], ACT.Copy,
                                     scale=SPLIT).then_inc(x_lo, 1)
            act.wait_ge(x_lo, 2)
            act.wait_ge(scalars_ready, 1)

            def step(first, count, _=None):
                base, delta = (nc.values_load_multi_w_load_instructions(
                    numbers[0:1, bass.ds(first, count)],
                    engines=[mybir.EngineType.Activation], min_val=0, max_val=most,
                    skip_runtime_bounds_check_because="they have been clipped")[1]
                    for numbers, most in ((base_i, N - 1), (delta_i, WINDOW - 1)))
                for j in range(count):
                    slot = j % DEPTH
                    act.wait_ge(joined, first + (j + 2))
                    nc.scalar.copy(carry[:, 1 - slot], counts_of(slot)[:, :, :, bass.ds(delta[j], 1)]
                                   ).then_inc(carried, 1)
                    act.wait_ge(copied, first + (j + 2))
                    window = A[:, :, bass.ds(base[j], WINDOW)].rearrange(
                        "p (a b) w -> p a b w", a=2)
                    nc.scalar.copy(window, counts_of(slot)).then_inc(copied, 1)

            def early_end(k):
                act.wait_ge(early_done, k + 1)
                act.wait_ge(early_free, k + 1)
                nc.scalar.activation(early_sum, ps[:, EARLY_LO], ACT.Copy, scale=1.0 / SPLIT
                                     ).then_inc(early_scaled, 1)

            def after_lead():
                act.wait_ge(rest_zeroed, 48)

            act.sem_inc(copied, 2)
            act.wait_ge(first_zeroed, 3)
            build(act, step, early_end=early_end, after_lead=after_lead)

            act.wait_ge(edges_checked, 1)
            for layer in range(3):
                to_table = (table1, table0, None)[layer]

                def lead(half, slot, nodes, layer=layer):
                    q = position(layer, half, slot)
                    if layer or 2 * half + slot >= EARLY:
                        act.wait_ge(agg_done, aggregated(layer, half, slot) + 1)
                        act.wait_ge(dense_done, q - 1)
                        act.wait_ge(lo_ready, q - 1 if layer < 2 else 2 * CHUNKS)
                        nc.scalar.activation(mean_T[:, slot, 0:nodes],
                                             ps[:, 2 * slot + 1, 0:nodes], ACT.Copy,
                                             scale=1.0 / SPLIT).then_inc(lo_scaled, 1)
                    act.wait_ge(turned, q + 1)
                    free(act, dense_done, q)
                    nc.scalar.copy(own_T[:, 0:nodes], ps[:, TURN, 0:nodes]
                                   ).then_inc(own_T_ready, 1)

                def post(half, slot, nodes, layer=layer, to_table=to_table):
                    q = position(layer, half, slot)
                    part = LAST if nodes == LAST else P
                    count = 1 if nodes == LAST else SUB
                    scratch = mean_T[:, slot].rearrange("p (t d) -> p t d", t=SUB)
                    if layer == 1:
                        act.wait_ge(dense_done, q + 1)
                        nc.scalar.activation(rows(scratch, nodes),
                                             dense_rows(DENSE + slot, nodes), ACT.Sigmoid
                                             ).then_inc(sigmoid_done, 1)
                    else:
                        act.wait_ge(ln_step, ln_steps(layer, half, slot) + 2)
                        free(act, rows_ready, q)
                        nc.scalar.activation(std[0:part, 0:count], moments[0:part, 0:count, 1],
                                             ACT.Sqrt, bias=eps_col[0:part]
                                             ).then_inc(std_ready, 1)
                    if layer < 2:
                        act.wait_ge(rows_ready, q + 1)
                        nc.scalar.activation(table_rows(to_table, half, slot, nodes, 0),
                                             rows(own[:, slot], nodes), ACT.Copy
                                             ).then_inc(hi_ready, 1)
                        act.wait_ge(rest_ready, q + 1)
                        nc.scalar.activation(table_rows(to_table, half, slot, nodes, 1),
                                             rows(scratch, nodes), ACT.Copy, scale=SPLIT
                                             ).then_inc(lo_ready, 1)

                lead_and_post(act, layer, lead, post)
            general_scalar(act)

        @block.tensor
        def _(pe):
            def count(group, slot):
                pe.wait_ge(v_hot, group + 1)
                pe.wait_ge(p_hot, group + 2)
                pe.wait_ge(copied, group + 1)
                cut = HALF * WINDOW
                low, high = 2 * slot, 2 * slot + 1
                for t in range(GROUP):
                    first = t == 0
                    nc.tensor.matmul(ps[:, low, 0:cut], LOW[:, slot, t], M[:, slot, t, 0:cut],
                                     start=first, stop=not first, skip_group_check=True)
                    nc.tensor.matmul(ps[:, high, 0:COMBINED - cut], LOW[:, slot, t],
                                     M[:, slot, t, cut:COMBINED],
                                     start=first, stop=not first, skip_group_check=True)
                    last = nc.tensor.matmul(ps[:, high, COMBINED - cut:cut],
                                            TYPE[:, slot, t], WIN[:, slot, t],
                                            start=False, stop=not first, skip_group_check=True)
                last.then_inc(counted, 1)

            def multiply(b, chunk_at):
                edge = isinstance(b, int)
                for part, bank in ((0, EARLY_HI), (1, EARLY_LO)):
                    block_at = b if edge else bass.ds(b, 1)
                    stationary = table0[:, block_at, part, :]
                    moving = A[:, block_at, chunk_at]
                    if not edge:
                        stationary, moving = stationary.squeeze(1), moving.squeeze(1)
                    last = nc.tensor.matmul(ps[:, bank, :], stationary, moving,
                                            start=edge and b == 0, stop=edge and b > 0,
                                            skip_group_check=True)
                return last

            def early_start(k):
                pe.wait_ge(early_summed, k + 1)
                multiply(0, columns_of(k))

            def early_end(k):
                multiply(ROWS - 1, columns_of(k)).then_inc(early_done, 1)

            def columns_of(k):
                return bass.ds(k * CHUNK, CHUNK) if not isinstance(k, int) else slice(
                    k * CHUNK, (k + 1) * CHUNK)

            def step(first, count_of_groups, early_block=None):
                for j in range(count_of_groups):
                    count(first + j, j % DEPTH)
                    if early_block:
                        early_block(j)

            pe.wait_ge(x_lo, 2)
            build(pe, step, early_start, lambda k, b: multiply(b, columns_of(k)), early_end)

            pe.wait_ge(copied, GROUPS + 2)
            pe.wait_ge(early_summed, EARLY + 1)
            pe.wait_ge(constants, 8)
            pe.wait_ge(weights_in, 16 * 10)

            def aggregate(layer, half, slot, nodes):
                table = (table0, table1, table0)[layer]
                blocks = ROWS if layer == 0 else BLOCKS
                at = nodes_at(half, slot, nodes)
                for part in range(2):
                    for b in range(blocks):
                        last = nc.tensor.matmul(ps[:, 2 * slot + part, 0:nodes],
                                                table[:, b, part, :], A[:, b, at],
                                                start=b == 0, stop=b == blocks - 1)
                last.then_inc(agg_done, 1)

            for chunk in range(EARLY, CHUNKS):
                aggregate(0, chunk // 2, chunk % 2, CHUNK if chunk < CHUNKS - 1 else LAST)
            pe.wait_ge(work_zeroed, 1)
            for layer in range(3):
                if layer:
                    pe.wait_ge(lo_ready, layer * CHUNKS)

                def lead(half, slot, nodes, layer=layer):
                    q = position(layer, half, slot)
                    if layer:
                        pe.wait_ge(summed, aggregated(layer, half, slot) - 1)
                        aggregate(layer, half, slot, nodes)
                    else:
                        free(pe, rdeg_ready, q)
                        nc.tensor.matmul(ps[:, DEG, 0:nodes], ones_h[:],
                                         A[:, BLOCKS, nodes_at(half, slot, nodes)],
                                         start=True, stop=True).then_inc(deg_done, 1)

                def turn(half, slot, nodes, layer=layer):
                    pe.wait_ge(own_loaded[slot], before(layer, half, slot) * 16 + 16)
                    free(pe, own_T_ready, position(layer, half, slot))
                    for t in range(1 if nodes == LAST else SUB):
                        size = min(P, nodes)
                        last = nc.tensor.transpose(ps[:, TURN, t * P:t * P + size],
                                                   own[0:size, slot, t, :],
                                                   ident[0:size, 0:size])
                    last.then_inc(turned, 1)

                def post(half, slot, nodes, layer=layer):
                    q = position(layer, half, slot)
                    pe.wait_ge(mean_ready, q + 1)
                    pe.wait_ge(own_T_ready, q + 1)
                    pe.wait_ge(y_ready, q + 1)
                    keep = 33 if layer == 0 else 1
                    for t in range(1 if nodes == LAST else SUB):
                        size = min(P, nodes)
                        at = slice(t * P, t * P + size)
                        to = ps[0:size, DENSE + slot, t * D:(t + 1) * D]
                        nc.tensor.matmul(to, mean_T[:, slot, at], weights[:, 2 * layer, :],
                                         start=True, stop=False)
                        nc.tensor.matmul(to, own_T[:, at], weights[:, 2 * layer + 1, :],
                                         start=False, stop=False)
                        last = nc.tensor.matmul(to, bias_rows[0:keep, at],
                                                bias[0:keep, layer, :],
                                                start=False, stop=True)
                    last.then_inc(dense_done, 1)

                if layer == 2:
                    pe.wait_ge(any_ready, 1)
                    nc.tensor.matmul(ps[0:1, DEG, 0:1], any_over, ones_col,
                                     start=True, stop=True).then_inc(over_counted, 1)
                lead_and_post(pe, layer, lead, post, turn)
            general_tensor(pe)

        @block.vector
        def _(dve):
            nc.vector.memset(stage_x[:, BLOCKS - 1:ROWS, :], 0.0).then_inc(pads_zero, 1)
            nc.vector.memset(zeros, 0.0).then_inc(zeros_ready, 1)
            nc.vector.memset(carry[:], 0.0).then_inc(carried, 1)
            nc.vector.memset(edge_f[:, TILES:PADDED, :], -1.0)
            nc.vector.memset(delta_i[:, GROUPS - 1:GROUPS], 0)
            nc.vector.memset(peaks, 0.0)
            nc.vector.memset(limits[:, 0:1], (WINDOW - 1) / 2)
            nc.vector.memset(limits[:, 1:2], 0.0)
            nc.vector.memset(limits[:, 2:3], MOST_VALUE)
            nc.vector.memset(limits[:, 3:3 + CHUNKS], MOST_EDGES - 1)
            nc.vector.memset(limits[:, 3 + CHUNKS:PEAKS], MOST_VALUE)
            nc.vector.memset(floors[:, 0:LEAD - DEPTH], 0.0)
            for k in range(EARLY):
                end = LEAD - DEPTH + (k + 1) * PERIOD if k < EARLY - 1 else GROUPS
                nc.vector.memset(floors[:, LEAD - DEPTH + k * PERIOD:end],
                                 float(CHUNK * (k + 1)))
            nc.vector.engine_nop().then_inc(edge_step, 1)
            dve.wait_ge(edge_step, 1)
            nc.vector.memset(floors[:, GROUPS - 1:GROUPS], float(N - WINDOW)
                             ).then_inc(edge_step, 1)
            zero_first(nc.vector.memset, 17, ROWS)
            nc.vector.engine_nop().then_inc(counted, 2)
            nc.vector.engine_nop().then_inc(joined, 1)
            nc.vector.engine_nop().then_inc(early_summed, 1)
            nc.vector.engine_nop().then_inc(early_free, 1)
            nc.vector.engine_nop().then_inc(y_ready, 2)

            dve.wait_ge(edges_in, 64)
            nc.vector.memset(first_i[:, 0:1], 0)
            nc.vector.tensor_scalar(low_i, src_i, P - 1, None, ALU.bitwise_and)
            nc.vector.tensor_scalar(block_i, src_i, P.bit_length() - 1, None,
                                    ALU.arith_shift_right)
            nc.vector.tensor_scalar(type_f, type_i, 0, RELATIONS - 1, ALU.max, ALU.min
                                    ).then_inc(edge_step, 1)
            dve.wait_ge(edge_step, 3)
            nc.vector.tensor_tensor(base_i, floors, first_i, ALU.max).then_inc(edge_step, 1)
            nc.vector.tensor_copy(low_f[:, 0:TILES], low_i)
            dve.wait_ge(edge_step, 4)
            nc.vector.tensor_scalar(base_i[:, 0:LEAD], base_i[:, 0:LEAD], QUARTER - WINDOW, None,
                                    ALU.min).then_inc(edge_step, 1)
            dve.wait_ge(edge_step, 5)
            nc.vector.tensor_tensor(offset_f.rearrange("p (g t) -> p g t", t=GROUP),
                                    dst_i.rearrange("p (g t) -> p g t", t=GROUP),
                                    base_i.unsqueeze(2).to_broadcast([P, GROUPS, GROUP]),
                                    ALU.subtract)
            nc.vector.tensor_tensor(delta_i[:, 0:GROUPS - 1], base_i[:, 1:GROUPS],
                                    base_i[:, 0:GROUPS - 1], ALU.subtract
                                    ).then_inc(edge_step, 1)
            dve.wait_ge(edge_step, 6)
            nc.vector.scalar_tensor_tensor(combined_f, block_i, float(WINDOW), offset_f,
                                           ALU.mult, ALU.add)
            nc.vector.tensor_scalar(delta_i, delta_i, 0, WINDOW - 1, ALU.max, ALU.min
                                    ).then_inc(edge_step, 1)
            dve.wait_ge(edge_step, 7)
            nc.vector.engine_nop().then_inc(scalars_ready, 1)
            for k in range(2):
                half = slice(k * HALF, (k + 1) * HALF)
                dve.wait_ge(x_hi, k + 1)
                nc.vector.tensor_tensor(stage_x[:, half], stage_x[:, half],
                                        table0[:, half, 0, :], ALU.subtract
                                        ).then_inc(x_rest, 1)
            dve.wait_ge(constants, 8)

            def one_hots(group, slot):
                tile = group * GROUP
                nc.vector.tensor_tensor(
                    WIN[:, slot],
                    iota_p[:, 0:WINDOW].unsqueeze(1).to_broadcast([P, GROUP, WINDOW]),
                    edge_f[:, columns(tile), 2:3].to_broadcast([P, GROUP, WINDOW]),
                    ALU.is_equal)
                if slot == 1:
                    nc.vector.tensor_scalar(LOW[:, slot, 1], iota_p,
                                            edge_f[:, column(tile + 1), 1], None, ALU.is_equal)
                for t in range(GROUP):
                    nc.vector.tensor_scalar(TYPE[:, slot, t], iota_p,
                                            edge_f[:, column(tile + t), 3], None, ALU.is_equal)
                    last = nc.vector.tensor_scalar(M[:, slot, t], iota_c,
                                                   edge_f[:, column(tile + t), 0],
                                                   None, ALU.is_equal)
                last.then_inc(v_hot, 1)

            def join(group, slot):
                dve.wait_ge(counted, group + 3)
                dve.wait_ge(carried, group + 1)
                first = counts_of(slot)[:, :, :, 0:1]
                nc.vector.tensor_tensor(first, first, carry[:, slot], ALU.add
                                        ).then_inc(joined, 1)

            def step(first, count, _=None):
                for j in range(count):
                    one_hots(first + (j + 1), (j + 1) % DEPTH)
                    join(first + j, j % DEPTH)

            def early_end(k):
                dve.wait_ge(early_scaled, k + 1)
                nc.vector.tensor_tensor(early_sum, ps[:, EARLY_HI], early_sum, ALU.add
                                        ).then_inc(early_summed, 1)

            one_hots(0, 0)
            build(dve, step, early_end=early_end)

            dve.wait_ge(counted, GROUPS + 2)
            dve.wait_ge(v_hot, GROUPS + 1)
            middle = -(WINDOW - 1) / 2
            rest = E - FULL_TILES * P
            nc.vector.memset(off_middle[:, FULL_TILES:TILES], 0.0)
            nc.vector.memset(late[:, TILES - GROUP:TILES], 0.0).then_inc(check_step, 1)
            dve.wait_ge(check_step, 1)
            nc.vector.tensor_scalar(off_middle[:, 0:FULL_TILES], offset_f[:, 0:FULL_TILES],
                                    middle, None, ALU.add)
            nc.vector.tensor_scalar(off_middle[0:rest, FULL_TILES:TILES],
                                    offset_f[0:rest, FULL_TILES:TILES], middle, None, ALU.add)
            nc.vector.tensor_tensor(off_middle[:, TILES:TILES + GROUPS - 1],
                                    base_i[:, 1:GROUPS], base_i[:, 0:GROUPS - 1],
                                    ALU.subtract).then_inc(check_step, 1)
            dve.wait_ge(check_step, 2)
            steps = off_middle[:, TILES:TILES + GROUPS - 1]
            nc.vector.tensor_tensor(
                late[:, 0:TILES - GROUP].rearrange("p (g t) -> p g t", t=GROUP),
                offset_f[:, 0:TILES - GROUP].rearrange("p (g t) -> p g t", t=GROUP),
                steps.unsqueeze(2).to_broadcast([P, GROUPS - 1, GROUP]), ALU.subtract
            ).then_inc(check_step, 1)
            dve.wait_ge(check_step, 3)
            nc.vector.tensor_scalar(steps, steps, middle, None, ALU.add)
            nc.vector.tensor_reduce(peaks[:, 1:2], late, AX.X, ALU.max)
            nc.vector.tensor_reduce(peaks[:, 2:3], table0[:, :, 0, :], AX.XY, ALU.max,
                                    apply_absolute_value=True).then_inc(check_step, 1)
            dve.wait_ge(check_step, 4)
            nc.vector.tensor_reduce(peaks[:, 0:1], off_middle[:, 0:TILES + GROUPS - 1], AX.X,
                                    ALU.max, apply_absolute_value=True
                                    ).then_inc(edges_checked, 1)

            dve.wait_ge(edges_checked, 1)
            dve.wait_ge(copied, GROUPS + 2)
            dve.wait_ge(early_stored, 16 * EARLY)
            nc.vector.memset(table1[:, BLOCKS - 1], 0.0)
            nc.vector.memset(bias_rows_all, 0.0).then_inc(bias_zero, 1)
            dve.wait_ge(bias_zero, 1)
            nc.vector.memset(bias_rows[0:1, :], 1.0).then_inc(work_zeroed, 1)
            dve.wait_ge(work_zeroed, 1)

            def peak(which, half, slot):
                return column(3 + which * CHUNKS + half * 2 + slot)

            for layer in range(3):
                def lead(half, slot, nodes, layer=layer):
                    q = position(layer, half, slot)
                    if layer == 0:
                        dve.wait_ge(deg_done, q + 1)
                        free(dve, rdeg_stored, q * 16)
                        free(dve, mean_ready, q)
                        nc.vector.tensor_reduce(peaks[:, peak(0, half, slot)],
                                                ps[:, DEG, 0:nodes], AX.X, ALU.max)
                        nc.vector.tensor_scalar(rdeg[:, 0:nodes], ps[:, DEG, 0:nodes], 1.0, None,
                                                ALU.max).then_inc(rdeg_step, 1)
                        free(dve, dense_done, q)
                        nc.vector.tensor_scalar(bias_rows[32:33, 0:nodes],
                                                ps[32:33, DEG, 0:nodes], 1.0, None, ALU.min
                                                ).then_inc(rdeg_step, 1)
                        dve.wait_ge(rdeg_step, q * 2 + 2)
                        nc.vector.reciprocal(rdeg[:, 0:nodes], rdeg[:, 0:nodes]
                                             ).then_inc(rdeg_ready, 1)
                    if layer or 2 * half + slot >= EARLY:
                        a = aggregated(layer, half, slot)
                        dve.wait_ge(lo_scaled, a + 1)
                        nc.vector.tensor_tensor(mean_T[:, slot, 0:nodes],
                                                ps[:, 2 * slot, 0:nodes],
                                                mean_T[:, slot, 0:nodes], ALU.add
                                                ).then_inc(summed, 1)
                        dve.wait_ge(summed, a + 1)
                    else:
                        dve.wait_ge(sum_loaded[slot], 16 * half + 16)
                    if layer == 0:
                        dve.wait_ge(rdeg_ready, q + 1)
                    else:
                        dve.wait_ge(rdeg_loaded, (q - (CHUNKS - 1)) * 16)
                    nc.vector.tensor_tensor(mean_T[:, slot, 0:nodes], mean_T[:, slot, 0:nodes],
                                            rdeg[:, 0:nodes], ALU.mult
                                            ).then_inc(mean_ready, 1)

                def post(half, slot, nodes, layer=layer):
                    q = position(layer, half, slot)
                    size = min(P, nodes)
                    count = 1 if nodes == LAST else SUB
                    mine = own[:, slot]
                    scratch = mean_T[:, slot].rearrange("p (t d) -> p t d", t=SUB)
                    dve.wait_ge(dense_done, q + 1)
                    if layer == 1:
                        dve.wait_ge(sigmoid_done, half * 2 + (slot + 1))
                        nc.vector.tensor_tensor(rows(mine, nodes),
                                                dense_rows(DENSE + slot, nodes),
                                                rows(scratch, nodes), ALU.mult
                                                ).then_inc(rows_ready, 1)
                    else:
                        before_it = mine if layer == 0 else residual
                        if layer == 2:
                            dve.wait_ge(residual_loaded, (half * 2 + (slot + 1)) * 16)
                        nc.vector.tensor_tensor(rows(mine, nodes),
                                                dense_rows(DENSE + slot, nodes),
                                                rows(before_it, nodes), ALU.add
                                                ).then_inc(y_ready, 1)
                        dve.wait_ge(y_ready, q + 3)
                        step = ln_steps(layer, half, slot)
                        for t in range(count):
                            last = nc.vector.bn_stats(stats[0:size, t], mine[0:size, t])
                        last.then_inc(ln_step, 1)
                        dve.wait_ge(ln_step, step + 1)
                        free(dve, rows_ready, q)
                        dve.sem_inc(waited, 1)
                        for t in range(count):
                            last = nc.vector.bn_aggr(moments[0:size, t], stats[0:size, t])
                        last.then_inc(ln_step, 1)
                        dve.wait_ge(std_ready, ln_chunks(layer, half, slot) + 1)
                        nc.vector.reciprocal(std[0:size, 0:count], std[0:size, 0:count]
                                             ).then_inc(ln_step, 1)
                        dve.wait_ge(ln_step, step + 3)
                        for t in range(count):
                            last = nc.vector.tensor_scalar(
                                mine[0:size, t], mine[0:size, t], moments[0:size, t, 0:1],
                                std[0:size, t:t + 1], ALU.subtract, ALU.mult)
                        last.then_inc(rows_ready, 1)
                    if layer < 2:
                        dve.wait_ge(rows_ready, q + 1)
                        if layer == 1:
                            values = mine[0:size, 0:count]
                            nc.vector.tensor_reduce(peaks[0:size, peak(1, half, slot)], values,
                                                    AX.XY, ALU.max, apply_absolute_value=True
                                                    ).then_inc(y_ready, 1)
                        dve.wait_ge(hi_ready, q + 1)
                        nc.vector.tensor_tensor(
                            rows(scratch, nodes), rows(mine, nodes),
                            table_rows((table1, table0)[layer], half, slot, nodes, 0),
                            ALU.subtract).then_inc(rest_ready, 1)

                if layer == 2:
                    dve.wait_ge(y_ready, 2 * CHUNKS + 2)
                    nc.vector.tensor_tensor(over, peaks, limits, ALU.is_gt).then_inc(over_step, 1)
                    dve.wait_ge(over_step, 1)
                    nc.vector.tensor_reduce(any_over, over, AX.X, ALU.max).then_inc(any_ready, 1)
                    dve.wait_ge(over_counted, 1)
                    nc.vector.tensor_copy(flag[0:1, :], ps[0:1, DEG, 0:1]).then_inc(flag_ready, 1)
                lead_and_post(dve, layer, lead, post)
            general_vector(dve)


def kernel(**inputs):
    import concourse.bacc as bacc
    from concourse.bass_utils import run_bass_kernel_spmd

    arrays = {}

    def lay(name, array):
        arrays[name] = np.ascontiguousarray(array)

    def edges(a, pad):
        a = np.asarray(a)
        padded = np.full(TILES * P, pad, a.dtype)
        padded[0:E] = a
        return padded.reshape(TILES, P).T

    dst = edges(inputs["dst"], NO_NODE)
    lay("x", inputs["x"])
    lay("src_t", edges(inputs["src"], 0))
    lay("dst_t", dst)
    lay("type_t", edges(inputs["edge_type_64"], 0))
    lay("first_dst", dst[0, ::GROUP])
    lay("rel_emb", inputs["L0_gnn_rel_emb"])
    for name, given in (("w_msg", "L0_gnn_W_msg"), ("w_self", "L0_gnn_W_self"),
                        ("w1_l", "L1_gnn_W1_l"), ("w1_r", "L1_gnn_W1_r"),
                        ("w2_l", "L1_gnn_W2_l"), ("w2_r", "L1_gnn_W2_r")):
        lay(name, np.asarray(inputs[given]).T)
    for name, given in (("b_self", "L0_gnn_b_self"), ("b_msg", "L0_gnn_b_msg"),
                        ("b1", "L1_gnn_b1"), ("b2", "L1_gnn_b2")):
        lay(name, np.asarray(inputs[given]).reshape(1, D))

    nc = bacc.Bacc("TRN2", target_bir_lowering=False, num_devices=1)
    args = {name: nc.dram_tensor(name, a.shape, mybir.dt.from_np(a.dtype),
                                 kind="ExternalInput").ap() for name, a in arrays.items()}
    for name, shape in (("x1_dram", (N, D)), ("h_dram", (N, D)), ("rdeg_dram", (P, N)),
                        ("sum_dram", (P, EARLY * CHUNK))):
        args[name] = nc.dram_tensor(name, shape, F32, kind="Internal").ap()
    args["out"] = nc.dram_tensor("out", (N, D), F32, kind="ExternalOutput").ap()
    gnn_program(nc, **args)
    return run_bass_kernel_spmd(nc, [arrays], core_ids=[0]).results[0]["out"]
```

```python
from contextlib import ExitStack

import numpy as np

import concourse.bass as bass
from concourse import mybir

ALU = mybir.AluOpType
ACT = mybir.ActivationFunctionType
AX = mybir.AxisListType
F32 = mybir.dt.float32
F16 = mybir.dt.float16
I32 = mybir.dt.int32
U32 = mybir.dt.uint32
DVE = mybir.EngineType.DVE

P = 128
N = 3125
D = 128
E = 53125
RELATIONS = 64
TILES = 416
FULL_TILES = E // P
GROUP = 2
GROUPS = TILES // GROUP
DEPTH = 2
WINDOW = 24
BLOCKS = (N + P - 1) // P
ROWS = BLOCKS + 1
HALF = ROWS // 2
COMBINED = BLOCKS * WINDOW
WIDTH = 3152
QUARTER = WIDTH // 4
CHUNK = 512
CHUNKS = (N + CHUNK - 1) // CHUNK
LAST = N - CHUNK * (CHUNKS - 1)
SUB = CHUNK // P
SPLIT = 2048.0
EARLY = 5
PERIOD = 34
LEAD = 40
UNROLL = 8
EARLY_GROUPS = ROWS - 2
MOST_EDGES = 2048.0
MOST_VALUE = 60000.0
PEAKS = 4 + CHUNKS
EPS = 1e-5
NO_NODE = 4096
assert LEAD % 4 == EARLY_GROUPS % UNROLL == GROUPS % UNROLL == ROWS % 2 == 0
assert LEAD + PERIOD * (EARLY - 1) + EARLY_GROUPS + DEPTH < GROUPS
assert WIDTH % 8 == 0 and WIDTH >= N - 1 + WINDOW and HALF * WINDOW <= 512
assert LAST <= P and CHUNKS == 7


def gnn_program(nc, x, src_t, dst_t, type_t, first_dst, rel_emb, w_msg, w_self, w1_l, w1_r,
                w2_l, w2_r, b_self, b_msg, b1, b2, x1_dram, h_dram, sum_dram, out):
    with ExitStack() as ctx:
        def sb(name, shape, dtype=F32):
            return ctx.enter_context(nc.sbuf_tensor(name, shape, dtype))

        def sem(name):
            return ctx.enter_context(nc.semaphore(name))

        A = sb("counts", [P, ROWS, WIDTH], F16)
        table0 = sb("table0", [P, ROWS, 2, D], F16)
        weights = sb("weights", [P, 7, D])
        bias = sb("bias", [33, 4, D])
        ident = sb("ident", [P, P])
        ones_h = sb("ones_h", [P, P], F16)
        eps_col = sb("eps_col", [P, 1])

        WORK = 7232
        work = sb("work", [P, WORK])

        def view(at, count, dtype=F32):
            words = count * (2 if dtype == F16 else 4) // 4
            assert at + words <= WORK, (at, words)
            piece = work[:, at:at + words]
            return (piece if dtype == F32 else piece.bitcast(dtype)), at + words

        at = 0
        iota_c, at = view(at, COMBINED, F16)
        iota_p, at = view(at, P, F16)
        PADDED = TILES + 2 * GROUP
        flat, at = view(at, PADDED * 4)
        edge_f = flat.rearrange("p (t k) -> p t k", k=4)
        combined_f, offset_f, type_f = (edge_f[:, 0:TILES, k] for k in (0, 2, 3))
        low_f = edge_f[:, :, 1]
        flat, at = view(at, DEPTH * GROUP)
        fetched = flat.rearrange("p (g t) -> p g t", g=DEPTH)
        base_i, at = view(at, GROUPS, I32)
        delta_i, at = view(at, GROUPS, I32)
        flat, at = view(at, DEPTH * ROWS)
        carry = flat.rearrange("p (s a b w) -> p s a b w", s=DEPTH, a=2, w=1)
        M_AT = at
        hot, at = view(at, DEPTH * GROUP * COMBINED, F16)
        M = hot.rearrange("p (g t c) -> p g t c", g=DEPTH, t=GROUP)
        hot, at = view(at, DEPTH * GROUP * P, F16)
        LOW = hot.rearrange("p (g t c) -> p g t c", g=DEPTH, t=GROUP)
        hot, at = view(at, DEPTH * GROUP * P, F16)
        TYPE = hot.rearrange("p (g t c) -> p g t c", g=DEPTH, t=GROUP)
        hot, at = view(at, DEPTH * GROUP * WINDOW, F16)
        WIN = hot.rearrange("p (g t c) -> p g t c", g=DEPTH, t=GROUP)
        early_sum, at = view(at, CHUNK)
        build_end = at

        stage = A[:].rearrange("p b w -> p (b w)").bitcast(F32).rearrange(
            "p (b w) -> p b w", b=ROWS)
        at = WIDTH // 2 - D
        stage_x = stage[:, :, at:at + D]

        def staged(block, count):
            return stage[:, block, at - TILES:at - TILES + count].bitcast(I32)

        src_i, dst_i, type_i, block_i, low_i = (staged(block, TILES) for block in range(5))
        first_i = staged(5, GROUPS)
        floors = stage[:, 6, at - TILES:at - TILES + GROUPS]

        off_middle, late = (work[:, M_AT + k * (TILES + GROUPS):M_AT + (k + 1) * (TILES + GROUPS)
                                 ] for k in range(2))
        late = late[:, 0:TILES]
        assert (TILES + GROUPS) * 2 <= DEPTH * GROUP * (COMBINED + P) // 2

        at = 0
        second, at = view(at, BLOCKS * 2 * D, F16)
        table1 = second.rearrange("p (b s d) -> p b s d", b=BLOCKS, s=2)
        residual = work[:, 0:CHUNK].rearrange("p (t d) -> p t d", t=SUB)
        flat, at = view(at, 2 * CHUNK)
        new = flat.rearrange("p (s t d) -> p s t d", s=2, t=SUB)
        own_T, at = view(at, CHUNK)
        flat, at = view(at, CHUNK)
        scaled = flat.rearrange("p (t d) -> p t d", t=SUB)
        degree, at = view(at, BLOCKS)
        rdeg, at = view(at, BLOCKS)
        flat, at = view(at, SUB * 6)
        stats = flat.rearrange("p (t k) -> p t k", t=SUB)
        flat, at = view(at, SUB * 2)
        moments = flat.rearrange("p (t k) -> p t k", t=SUB)
        std, at = view(at, SUB)
        flat, at = view(at, 3 * D, F16)
        bias_h = flat[0:33].rearrange("p (k d) -> p k d", k=3)
        flat, at = view(at, P, F16)
        bias_scale = flat[0:33]
        at = max(at, build_end)
        flat, at = view(at, CHUNK)
        own = flat.rearrange("p (t d) -> p t d", t=SUB)
        zeros = flat[:, 0:QUARTER // 2]
        flat, at = view(at, 2 * CHUNK)
        sum_T = flat.rearrange("p (s n) -> p s n", s=2)
        peaks, at = view(at, PEAKS)
        limits, at = view(at, PEAKS)
        over, at = view(at, PEAKS)
        any_over, at = view(at, 1)
        ones_col, at = view(at, 1)
        flag, at = view(at, 1, I32)
        spare, at = view(at, 1)

        ps = ctx.enter_context(nc.psum_tensor("ps", [P, 8, 512], F32))
        MESSAGES, DENSE, DEG, TURN = 4, 5, 6, 7
        EARLY_HI, EARLY_LO = 4, 5

        edges_in = sem("edges_in")
        x_in = [sem(f"x_in{k}") for k in range(2)]
        weights_in = sem("weights_in")
        constants = sem("constants")
        pads_zero = sem("pads_zero")
        edge_step = sem("edge_step")
        scalars_ready = sem("scalars_ready")
        x_hi = sem("x_hi")
        x_rest = sem("x_rest")
        x_lo = sem("x_lo")
        v_hot = sem("v_hot")
        p_hot = sem("p_hot")
        p_fetched = sem("p_fetched")
        counted = sem("counted")
        joined = sem("joined")
        carried = sem("carried")
        zeros_ready = sem("zeros_ready")
        first_zeroed = sem("first_zeroed")
        rest_zeroed = sem("rest_zeroed")
        copied = sem("copied")
        early_done = sem("early_done")
        early_scaled = sem("early_scaled")
        early_summed = sem("early_summed")
        early_stored = sem("early_stored")
        early_free = sem("early_free")
        sum_loaded = [sem(f"sum_loaded{k}") for k in range(2)]
        waited = sem("waited")
        over_step = sem("over_step")
        any_ready = sem("any_ready")
        over_counted = sem("over_counted")
        flag_ready = sem("flag_ready")
        check_step = sem("check_step")
        deg_step = sem("deg_step")
        bias_step = sem("bias_step")
        edges_checked = sem("edges_checked")
        agg_done = sem("agg_done")
        deg_done = sem("deg_done")
        turned = sem("turned")
        weights_ready = sem("weights_ready")
        messages_done = sem("messages_done")
        messages_scaled = sem("messages_scaled")
        z_ready = sem("z_ready")
        dense_done = sem("dense_done")
        lo_scaled = sem("lo_scaled")
        own_T_ready = sem("own_T_ready")
        sigmoid_done = sem("sigmoid_done")
        std_ready = sem("std_ready")
        hi_ready = sem("hi_ready")
        lo_ready = sem("lo_ready")
        rdeg_ready = sem("rdeg_ready")
        summed = sem("summed")
        y_ready = sem("y_ready")
        ln_step = sem("ln_step")
        rows_ready = sem("rows_ready")
        rest_ready = sem("rest_ready")
        own_loaded = [sem(f"own_loaded{k}") for k in range(2)]
        residual_loaded = sem("residual_loaded")
        rows_stored = [sem(f"rows_stored{k}") for k in range(2)]

        IN_SLOT = [(CHUNKS + 1) // 2, CHUNKS // 2]

        def before(layer, half, slot):
            return layer * IN_SLOT[slot] + half

        def position(layer, half, slot):
            return layer * CHUNKS + half * 2 + slot

        def free(eng, semaphore, value):
            if not isinstance(value, int) or value > 0:
                eng.wait_ge(semaphore, value)

        def counts_of(slot):
            return ps[:, 2 * slot:2 * slot + 2, 0:HALF * WINDOW].rearrange(
                "p a (b w) -> p a b w", w=WINDOW)

        def aggregated(layer, half, slot):
            return position(layer, half, slot) - EARLY

        def lead_and_post(eng, layer, lead, post, turn=None, finish=None):
            turn = turn or (lambda *chunk: None)
            finish = finish or (lambda *chunk: None)
            last = CHUNKS // 2
            lead(0, 0, CHUNK)
            turn(0, 0, CHUNK)

            def pair(half):
                for now, then in (((half, 1, CHUNK), (half, 0, CHUNK)),
                                  ((half + 1, 0, CHUNK), (half, 1, CHUNK))):
                    lead(*now)
                    post(*then)
                    turn(*now)
                    finish(*then)

            pair(0)
            if layer == 0:
                for half in range(1, last - 1):
                    pair(half)
            else:
                with eng.Fori(1, last - 1) as half:
                    pair(half)
            lead(last - 1, 1, CHUNK)
            post(last - 1, 0, CHUNK)
            turn(last - 1, 1, CHUNK)
            finish(last - 1, 0, CHUNK)
            lead(last, 0, LAST)
            post(last - 1, 1, CHUNK)
            turn(last, 0, LAST)
            finish(last - 1, 1, CHUNK)
            post(last, 0, LAST)
            finish(last, 0, LAST)

        def nodes_at(half, slot, nodes):
            start = half * (2 * CHUNK) + slot * CHUNK
            return slice(start, start + nodes) if isinstance(start, int) else bass.ds(start, nodes)

        def dram_rows(dram, half, slot, nodes):
            rows = dram[nodes_at(half, slot, nodes), :]
            return rows if nodes == LAST else rows.rearrange("(t p) d -> p t d", p=P)

        def rows(buffer, nodes):
            return buffer[0:LAST, 0, :] if nodes == LAST else buffer

        def table_rows(table, half, slot, nodes, part):
            if nodes == LAST:
                return table[0:LAST, BLOCKS - 1, part, :]
            first = half * (2 * SUB) + slot * SUB
            span = slice(first, first + SUB) if isinstance(first, int) else bass.ds(first, SUB)
            return table[:, span, part, :]

        def dense_rows(bank, nodes):
            if nodes == LAST:
                return ps[0:LAST, bank, 0:D]
            return ps[:, bank, :].rearrange("p (t d) -> p t d", t=SUB)

        def column(tile):
            return slice(tile, tile + 1) if isinstance(tile, int) else bass.ds(tile, 1)

        def columns(tile):
            return slice(tile, tile + GROUP) if isinstance(tile, int) else bass.ds(tile, GROUP)

        def ln_chunks(layer, half, slot):
            return (0 if layer == 0 else CHUNKS) + half * 2 + slot

        def ln_steps(layer, half, slot):
            return ln_chunks(layer, half, slot) * 3

        free_words = A[:].rearrange("p b w -> p (b w)").bitcast(F32)

        def placed(at, count, dtype=F32):
            piece = free_words[:, at:at + count]
            return (piece if dtype == F32 else piece.bitcast(dtype)), at + count

        g_iota, at = placed(0, N)
        g_hot, at = placed(at, N)
        g_mean_T, at = placed(at, N)
        g_rdeg, at = placed(at, N)
        g_rows_of_bias, at = placed(at, N)
        g_bias_rows = g_rows_of_bias[0:33]
        g_src, at = placed(at, TILES, I32)
        g_dst, at = placed(at, TILES, I32)
        g_type, at = placed(at, TILES, I32)
        g_dst_f, at = placed(at, TILES)
        g_index, at = placed(at, 2, I32)
        g_ones, at = placed(at, P)
        g_source, at = placed(at, D)
        g_relation, at = placed(at, D)
        g_own, at = placed(at, D)
        g_residual, at = placed(at, D)
        g_own_T, at = placed(at, P)
        g_mean_tile, at = placed(at, P)
        g_bias_tile, at = placed(at, P)
        g_sigmoid, at = placed(at, D)
        g_new, at = placed(at, D)
        g_stats, at = placed(at, 6)
        g_moments, at = placed(at, 2)
        g_std, at = placed(at, 1)
        G_TURN, G_DENSE = slice(0, P), slice(P, P + D)

        gs_edges = sem("general_edges")
        gs_setup = sem("general_setup")
        gs_lists = sem("general_lists")
        gs_index = sem("general_index")
        gs_source = sem("general_source")
        gs_relation = sem("general_relation")
        gs_message = sem("general_message")
        gs_hot = sem("general_hot")
        gs_counted = sem("general_counted")
        gs_pass = sem("general_pass")
        gs_own = sem("general_own")
        gs_turned = sem("general_turned")
        gs_own_T = sem("general_own_T")
        gs_dense = sem("general_dense")
        gs_sigmoid = sem("general_sigmoid")
        gs_std = sem("general_std")
        gs_step = sem("general_step")
        gs_row = sem("general_row")
        gs_stored = sem("general_stored")

        def hold(eng, semaphore, value):
            if not isinstance(value, int) or value > 0:
                eng.wait_ge(semaphore, value)
                eng.sem_inc(waited, 1)

        def if_over(eng, engine_type, general):
            eng.wait_ge(flag_ready, 1)
            found = nc.values_load_multi_w_load_instructions(
                flag[0:1, 0:1], engines=[engine_type], min_val=0, max_val=P,
                skip_runtime_bounds_check_because="it counts partitions")[1][0]
            with eng.If(found != 0):
                for slot in range(2):
                    eng.wait_ge(rows_stored[slot], 16 * before(3, 0, slot))
                eng.sem_inc(waited, 1)
                general()

        def edge_tiles(eng, step):
            step(0, True)
            with eng.Fori(1, TILES) as tile:
                step(tile, False)

        def node_tiles(eng, step):
            step(0, P)
            with eng.Fori(1, BLOCKS - 1) as tile:
                step(tile, P)
            step(BLOCKS - 1, N - P * (BLOCKS - 1))

        def node_span(tile, size):
            return slice(tile * P, tile * P + size) if isinstance(tile, int) else bass.ds(
                tile * P, size)

        def general_sync(sp):
            def general():
                for to, given in ((g_src, src_t), (g_dst, dst_t), (g_type, type_t)):
                    sp.dma_start(to, given).then_inc(gs_edges, 16)
                for layer, (source, sink) in enumerate(((x, x1_dram), (x1_dram, h_dram),
                                                        (h_dram, out))):
                    def step(tile, size, layer=layer, source=source, sink=sink):
                        q = layer * BLOCKS + tile
                        span = node_span(tile, size)
                        hold(sp, gs_stored, q * 16)
                        sp.dma_start(g_own[0:size], source[span, :]).then_inc(gs_own, 16)
                        sp.dma_start(g_residual[0:size], (x1_dram if layer == 2 else source)
                                     [span, :]).then_inc(gs_own, 16)
                        hold(sp, gs_row, q + 1)
                        sp.dma_start(sink[span, :], g_new[0:size]).then_inc(gs_stored, 16)

                    node_tiles(sp, step)
                sp.wait_ge(gs_stored, 16 * 3 * BLOCKS)

            if_over(sp, mybir.EngineType.SP, general)

        def general_gpsimd(pool):
            def general():
                nc.gpsimd.iota(g_iota, [[1, N]], base=0, channel_multiplier=0,
                               allow_small_or_imprecise_dtypes=True).then_inc(gs_setup, 1)
                nc.gpsimd.memset(g_ones, 1.0).then_inc(gs_setup, 1)
                nc.gpsimd.memset(g_rows_of_bias, 0.0).then_inc(gs_setup, 1)
                pool.wait_ge(gs_setup, 3)
                nc.gpsimd.memset(g_rows_of_bias[0:1], 1.0).then_inc(gs_setup, 1)
                pool.wait_ge(gs_lists, 1)
                for layer, source in enumerate((x, x1_dram, h_dram)):
                    hold(pool, gs_stored, 16 * BLOCKS * layer)

                    def step(tile, _, layer=layer, source=source):
                        n = layer * TILES + tile
                        hold(pool, gs_counted, n + TILES)
                        nc.gpsimd.tensor_copy(g_index[:, 0:1], g_src[:, column(tile)]
                                              ).then_inc(gs_index, 1)
                        nc.gpsimd.tensor_copy(g_index[:, 1:2], g_type[:, column(tile)]
                                              ).then_inc(gs_index, 1)
                        hold(pool, gs_index, 2 * n + 2)
                        nc.gpsimd.indirect_dma_start(
                            g_source, None, source,
                            bass.IndirectOffsetOnAxis(ap=g_index[:, 0:1], axis=0)
                        ).then_inc(gs_source, 16)
                        if layer == 0:
                            nc.gpsimd.indirect_dma_start(
                                g_relation, None, rel_emb,
                                bass.IndirectOffsetOnAxis(ap=g_index[:, 1:2], axis=0)
                            ).then_inc(gs_relation, 16)

                    edge_tiles(pool, step)

            if_over(pool, mybir.EngineType.Pool, general)

        def general_scalar(act):
            def general():
                for layer in range(3):
                    act.wait_ge(gs_pass, layer + 2)

                    def step(tile, size, layer=layer):
                        q = layer * BLOCKS + tile
                        span = node_span(tile, size)
                        hold(act, gs_turned, q + 1)
                        nc.scalar.copy(g_mean_tile[:, 0:size], g_mean_T[:, span])
                        nc.scalar.copy(g_bias_tile[0:33, 0:size], g_bias_rows[:, span])
                        nc.scalar.copy(g_own_T[:, 0:size], ps[:, 7, 0:size]
                                       ).then_inc(gs_own_T, 1)
                        if layer == 1:
                            hold(act, gs_dense, q + 1)
                            nc.scalar.activation(g_sigmoid[0:size], ps[0:size, 7, G_DENSE],
                                                 ACT.Sigmoid).then_inc(gs_sigmoid, 1)
                        else:
                            normalised = (0 if layer == 0 else BLOCKS) + tile
                            hold(act, gs_step, normalised * 4 + 3)
                            nc.scalar.activation(g_std[0:size], g_moments[0:size, 1:2],
                                                 ACT.Sqrt, bias=eps_col[0:size]
                                                 ).then_inc(gs_std, 1)

                    node_tiles(act, step)

            if_over(act, mybir.EngineType.Activation, general)

        def general_tensor(pe):
            def general():
                pe.wait_ge(gs_setup, 4)
                for k in range(4):
                    hold(pe, gs_pass, k)
                    hold(pe, gs_row, BLOCKS * (k - 1))

                    def step(tile, first, k=k):
                        hold(pe, gs_hot, k * TILES + tile + 1)
                        if k == 1:
                            hold(pe, gs_message, tile + 1)
                        elif k > 1:
                            hold(pe, gs_source, ((k - 1) * TILES + tile) * 16 + 16)
                        for c in range(CHUNKS):
                            nodes = CHUNK if c < CHUNKS - 1 else LAST
                            last = nc.tensor.matmul(
                                ps[:, c, 0:nodes], g_source if k else g_ones,
                                g_hot[:, c * CHUNK:c * CHUNK + nodes],
                                start=first, stop=not first, skip_group_check=True)
                        last.then_inc(gs_counted, 1)

                    edge_tiles(pe, step)
                    if k == 0:
                        continue
                    hold(pe, gs_pass, k + 1)

                    def dense(tile, size, layer=k - 1):
                        q = layer * BLOCKS + tile
                        hold(pe, gs_own, q * 32 + 32)
                        nc.tensor.transpose(ps[:, 7, 0:size], g_own[0:size],
                                            ident[0:size, 0:size]).then_inc(gs_turned, 1)
                        hold(pe, gs_own_T, q + 1)
                        to = ps[0:size, 7, G_DENSE]
                        keep = 33 if layer == 0 else 1
                        nc.tensor.matmul(to, g_mean_tile[:, 0:size],
                                         weights[:, 2 * layer, :], start=True, stop=False)
                        nc.tensor.matmul(to, g_own_T[:, 0:size], weights[:, 2 * layer + 1, :],
                                         start=False, stop=False)
                        nc.tensor.matmul(to, g_bias_tile[0:keep, 0:size],
                                         bias[0:keep, layer, :],
                                         start=False, stop=True).then_inc(gs_dense, 1)

                    node_tiles(pe, dense)

            if_over(pe, mybir.EngineType.PE, general)

        def general_vector(dve):
            def general():
                dve.wait_ge(gs_edges, 48)
                nc.vector.tensor_copy(g_dst_f, g_dst)
                nc.vector.tensor_scalar(g_type, g_type, 0, RELATIONS - 1, ALU.max, ALU.min
                                        ).then_inc(gs_lists, 1)
                dve.wait_ge(gs_lists, 1)
                dve.wait_ge(gs_setup, 4)
                sums = ps[:].rearrange("p b c -> p (b c)")[:, 0:N]
                for k in range(4):
                    def step(tile, _, k=k):
                        n = k * TILES + tile
                        hold(dve, gs_counted, n)
                        nc.vector.tensor_scalar(g_hot, g_iota, g_dst_f[:, column(tile)], None,
                                                ALU.is_equal).then_inc(gs_hot, 1)
                        if k == 1:
                            hold(dve, gs_source, tile * 16 + 16)
                            hold(dve, gs_relation, tile * 16 + 16)
                            nc.vector.tensor_tensor(g_source, g_source, g_relation, ALU.add
                                                    ).then_inc(gs_message, 1)

                    edge_tiles(dve, step)
                    hold(dve, gs_counted, (k + 1) * TILES)
                    if k == 0:
                        nc.vector.tensor_scalar(g_rdeg, sums, 1.0, None, ALU.max)
                        nc.vector.tensor_scalar(g_bias_rows[32:33], sums[32:33], 1.0, None,
                                                ALU.min).then_inc(gs_lists, 1)
                        dve.wait_ge(gs_lists, 2)
                        nc.vector.reciprocal(g_rdeg, g_rdeg).then_inc(gs_pass, 1)
                        dve.wait_ge(gs_pass, 1)
                        continue
                    nc.vector.tensor_tensor(g_mean_T, sums, g_rdeg, ALU.mult
                                            ).then_inc(gs_pass, 1)

                    def rows_of(tile, size, layer=k - 1):
                        q = layer * BLOCKS + tile
                        y = g_new[0:size]
                        products = ps[0:size, 7, G_DENSE]
                        if layer == 1:
                            hold(dve, gs_sigmoid, tile + 1)
                            nc.vector.tensor_tensor(y, products, g_sigmoid[0:size], ALU.mult
                                                    ).then_inc(gs_row, 1)
                            return
                        done = ((0 if layer == 0 else BLOCKS) + tile) * 4
                        hold(dve, gs_dense, q + 1)
                        nc.vector.tensor_tensor(y, products, g_residual[0:size], ALU.add
                                                ).then_inc(gs_step, 1)
                        hold(dve, gs_step, done + 1)
                        nc.vector.bn_stats(g_stats[0:size], y).then_inc(gs_step, 1)
                        hold(dve, gs_step, done + 2)
                        nc.vector.bn_aggr(g_moments[0:size], g_stats[0:size]
                                          ).then_inc(gs_step, 1)
                        hold(dve, gs_std, (0 if layer == 0 else BLOCKS) + tile + 1)
                        nc.vector.reciprocal(g_std[0:size], g_std[0:size]
                                             ).then_inc(gs_step, 1)
                        hold(dve, gs_step, done + 4)
                        nc.vector.tensor_scalar(y, y, g_moments[0:size, 0:1], g_std[0:size],
                                                ALU.subtract, ALU.mult).then_inc(gs_row, 1)

                    node_tiles(dve, rows_of)

            if_over(dve, mybir.EngineType.DVE, general)

        def zero_first(memset, first_block, last_block):
            memset(A[:, first_block:last_block, 0:QUARTER].bitcast(U32), 0
                   ).then_inc(first_zeroed, 1)

        def build(eng, step, early_start=None, early_block=None, early_end=None,
                  after_lead=None):
            with eng.Fori(0, 2) as i:
                for at in range(0, LEAD // 2, UNROLL):
                    step(i * (LEAD // 2) + at, min(UNROLL, LEAD // 2 - at))
            if after_lead:
                after_lead()

            def period(k, length):
                if early_start:
                    early_start(k)
                first = k * PERIOD + LEAD
                for i in range(EARLY_GROUPS // UNROLL):
                    step(first + i * UNROLL, UNROLL,
                         early_block and (lambda j: early_block(k, i * UNROLL + (1 + j))))
                step(first + EARLY_GROUPS, DEPTH)
                if early_end:
                    early_end(k)
                step(first + (EARLY_GROUPS + DEPTH), length - EARLY_GROUPS - DEPTH)

            with eng.Fori(0, EARLY - 1) as k:
                period(k, PERIOD)
            period(EARLY - 1, GROUPS - LEAD - PERIOD * (EARLY - 1))

        block = ctx.enter_context(nc.Block())

        @block.sync
        def _(sp):
            cut = HALF * P
            full = (BLOCKS - 1) * P
            sp.dma_start(stage_x[:, 0:HALF, :], x[0:cut, :].rearrange("(b p) d -> p b d", p=P)
                         ).then_inc(x_in[0], 16)
            sp.dma_start(stage_x[:, HALF:BLOCKS - 1, :],
                         x[cut:full, :].rearrange("(b p) d -> p b d", p=P)
                         ).then_inc(x_in[1], 16)
            sp.wait_ge(pads_zero, 1)
            sp.dma_start(stage_x[0:N - full, BLOCKS - 1, :], x[full:N, :]).then_inc(x_in[1], 16)
            sp.dma_start(stage_x[0:RELATIONS, BLOCKS, :], rel_emb).then_inc(x_in[1], 16)
            sp.wait_ge(constants, 1)
            for k, w in enumerate((w_msg, w_self, w1_l, w1_r, w2_l, w2_r)):
                sp.dma_start(weights[:, k, :], w).then_inc(weights_in, 16)
            for row, k, b in ((0, 0, b_self), (32, 0, b_msg), (0, 1, b1), (0, 2, b2), (0, 3, b_msg),
                              (32, 1, b1), (32, 2, b2), (32, 3, b_self)):
                sp.dma_start(bias[row:row + 1, k, :], b).then_inc(weights_in, 16)

            for quarter in range(1, 4):
                if quarter == 1:
                    sp.wait_ge(zeros_ready, 1)
                elif quarter == 2:
                    sp.wait_ge(scalars_ready, 1)
                else:
                    sp.wait_ge(x_lo, 2)
                sp.dma_start(
                    A[:, :, quarter * QUARTER:(quarter + 1) * QUARTER].bitcast(F32),
                    zeros.unsqueeze(1).to_broadcast([P, ROWS, QUARTER // 2])
                ).then_inc(rest_zeroed, 16)

            with sp.Fori(0, EARLY) as k:
                sp.wait_ge(early_summed, k + 2)
                sp.sem_inc(waited, 1)
                sp.dma_start(sum_dram[:, bass.ds(k * CHUNK, CHUNK)], early_sum
                             ).then_inc(early_stored, 16)
                sp.wait_ge(early_stored, k * 16 + 16)
                sp.sem_inc(early_free, 1)

            for layer, (source, sink) in enumerate(((x, x1_dram), (x1_dram, h_dram),
                                                    (h_dram, out))):
                def load(half, slot, nodes, layer=layer, source=source):
                    free(sp, turned, position(layer, half, slot))
                    sp.dma_start(rows(own, nodes), dram_rows(source, half, slot, nodes)
                                 ).then_inc(own_loaded[slot], 16)

                def store(half, slot, nodes, layer=layer, sink=sink):
                    sp.wait_ge(rows_ready, position(layer, half, slot) + 1)
                    sp.dma_start(dram_rows(sink, half, slot, nodes), rows(new[:, slot], nodes)
                                 ).then_inc(rows_stored[slot], 16)

                def load_residual(half, slot, nodes):
                    sp.dma_start(rows(residual, nodes), dram_rows(x1_dram, half, slot, nodes)
                                 ).then_inc(residual_loaded, 16)

                if layer == 0:
                    sp.wait_ge(rest_zeroed, 48)
                else:
                    for slot in range(2):
                        sp.wait_ge(rows_stored[slot], before(layer, 0, slot) * 16)
                load(0, 0, CHUNK)
                load(0, 1, CHUNK)
                if layer == 2:
                    sp.wait_ge(agg_done, 2 * CHUNKS - EARLY)
                    load_residual(0, 0, CHUNK)
                with sp.Fori(0, 2) as half:
                    for slot in range(2):
                        load(half + 1, slot, CHUNK)
                        store(half, slot, CHUNK)
                        if layer == 2:
                            load_residual(*((half, 1) if slot == 0 else (half + 1, 0)), CHUNK)
                load(3, 0, LAST)
                store(2, 0, CHUNK)
                if layer == 2:
                    load_residual(2, 1, CHUNK)
                store(2, 1, CHUNK)
                if layer == 2:
                    load_residual(3, 0, LAST)
                store(3, 0, LAST)
            for slot in range(2):
                sp.wait_ge(rows_stored[slot], 16 * before(3, 0, slot))
            general_sync(sp)

        @block.gpsimd
        def _(pool):
            nc.gpsimd.memset(bias[:], 0.0).then_inc(constants, 1)
            nc.gpsimd.iota(iota_c, [[1, COMBINED]], base=0, channel_multiplier=0,
                           allow_small_or_imprecise_dtypes=True).then_inc(constants, 1)
            nc.gpsimd.iota(iota_p, [[1, P]], base=0, channel_multiplier=0,
                           allow_small_or_imprecise_dtypes=True).then_inc(constants, 1)
            nc.gpsimd.memset(ones_h[:], 1.0).then_inc(constants, 1)
            nc.gpsimd.memset(eps_col[:], EPS).then_inc(constants, 1)
            nc.gpsimd.memset(ident[:], 0.0).then_inc(constants, 1)
            nc.gpsimd.memset(ones_col, 1.0).then_inc(constants, 1)
            pool.wait_ge(constants, 7)
            nc.gpsimd.affine_select(out=ident[:], in_=ident[:], compare_op=ALU.not_equal,
                                    fill=1.0, base=0, pattern=[[-1, P]],
                                    channel_multiplier=1).then_inc(constants, 1)
            zero_first(nc.gpsimd.memset, 0, 8)
            pool.wait_ge(scalars_ready, 1)

            def fetch(group, slot):
                nc.gpsimd.tensor_copy(fetched[:, slot], low_f[:, columns(group * GROUP)]
                                      ).then_inc(p_fetched, 1)

            def one_hots(group, slot):
                pool.wait_ge(p_fetched, group + 1)
                pool.wait_ge(p_hot, group + 1)
                fetch(group + 1, 1 - slot)
                for t in range(GROUP - slot):
                    last = nc.gpsimd.tensor_scalar(LOW[:, slot, t], iota_p,
                                                   fetched[:, slot, t:t + 1], None, ALU.is_equal)
                last.then_inc(p_hot, 1)

            pool.sem_inc(p_hot, 1)
            fetch(0, 0)
            with pool.Fori(0, GROUPS // UNROLL) as i:
                for j in range(UNROLL):
                    pool.wait_ge(counted, i * UNROLL + (j + 1))
                    one_hots(i * UNROLL + j, j % DEPTH)

            pool.wait_ge(early_stored, 16 * EARLY)

            def load_sum(chunk):
                half, slot = divmod(chunk, 2)
                free(pool, messages_done, chunk - 1)
                pool.dma_start(sum_T[:, slot], sum_dram[:, nodes_at(half, slot, CHUNK)]
                               ).then_inc(sum_loaded[slot], 16)

            for chunk in range(EARLY):
                load_sum(chunk)
            general_gpsimd(pool)

        @block.scalar
        def _(act):
            for to, given in ((dst_i, dst_t), (src_i, src_t), (type_i, type_t)):
                act.dma_start(to, given).then_inc(edges_in, 16)
            act.dma_start(first_i, first_dst.partition_broadcast(P)).then_inc(edges_in, 16)
            zero_first(lambda out, _: nc.scalar.memzero(out), 8, 17)
            halves = [slice(k * HALF, (k + 1) * HALF) for k in range(2)]
            for k, half in enumerate(halves):
                act.wait_ge(x_in[k], (16, 48)[k])
                nc.scalar.activation(table0[:, half, 0, :], stage_x[:, half], ACT.Copy
                                     ).then_inc(x_hi, 1)
            for k, half in enumerate(halves):
                act.wait_ge(x_rest, k + 1)
                nc.scalar.activation(table0[:, half, 1, :], stage_x[:, half], ACT.Copy,
                                     scale=SPLIT).then_inc(x_lo, 1)
            act.wait_ge(x_lo, 2)
            act.wait_ge(scalars_ready, 1)

            def step(first, count, _=None):
                base, delta = (nc.values_load_multi_w_load_instructions(
                    numbers[0:1, bass.ds(first, count)],
                    engines=[mybir.EngineType.Activation], min_val=0, max_val=most,
                    skip_runtime_bounds_check_because="they have been clipped")[1]
                    for numbers, most in ((base_i, N - 1), (delta_i, WINDOW - 1)))
                for j in range(count):
                    slot = j % DEPTH
                    act.wait_ge(joined, first + (j + 2))
                    nc.scalar.copy(carry[:, 1 - slot],
                                   counts_of(slot)[:, :, :, bass.ds(delta[j], 1)]
                                   ).then_inc(carried, 1)
                    act.wait_ge(copied, first + (j + 2))
                    window = A[:, :, bass.ds(base[j], WINDOW)].rearrange(
                        "p (a b) w -> p a b w", a=2)
                    nc.scalar.copy(window, counts_of(slot)).then_inc(copied, 1)

            def early_end(k):
                act.wait_ge(early_done, k + 1)
                act.wait_ge(early_free, k + 1)
                nc.scalar.activation(early_sum, ps[:, EARLY_LO], ACT.Copy, scale=1.0 / SPLIT
                                     ).then_inc(early_scaled, 1)

            def after_lead():
                act.wait_ge(rest_zeroed, 48)

            act.sem_inc(copied, 2)
            act.wait_ge(first_zeroed, 3)
            build(act, step, early_end=early_end, after_lead=after_lead)

            act.wait_ge(edges_checked, 1)
            for layer in range(3):
                to_table = (table1, table0, None)[layer]

                def lead(half, slot, nodes, layer=layer):
                    q = position(layer, half, slot)
                    if layer or 2 * half + slot >= EARLY:
                        act.wait_ge(agg_done, aggregated(layer, half, slot) + 1)
                        act.wait_ge(messages_done, q - 1)
                        nc.scalar.activation(sum_T[:, slot, 0:nodes],
                                             ps[:, 2 * slot + 1, 0:nodes], ACT.Copy,
                                             scale=1.0 / SPLIT).then_inc(lo_scaled, 1)

                def turn(half, slot, nodes, layer=layer):
                    q = position(layer, half, slot)
                    act.wait_ge(turned, q + 1)
                    free(act, dense_done, q)
                    nc.scalar.copy(own_T[:, 0:nodes], ps[:, TURN, 0:nodes]
                                   ).then_inc(own_T_ready, 1)

                def post(half, slot, nodes, layer=layer, to_table=to_table):
                    q = position(layer, half, slot)
                    part = LAST if nodes == LAST else P
                    count = 1 if nodes == LAST else SUB
                    act.wait_ge(messages_done, q + 1)
                    act.wait_ge(y_ready, q + 2)
                    act.sem_inc(waited, 1)
                    free(act, lo_ready, q if layer < 2 else 2 * CHUNKS)
                    act.sem_inc(waited, 1)
                    for t in range(count):
                        last = nc.scalar.activation(
                            scaled[0:part, t], ps[0:part, MESSAGES, t * D:(t + 1) * D], ACT.Copy,
                            scale=rdeg[0:part, column(half * (2 * SUB) + slot * SUB + t)])
                    last.then_inc(messages_scaled, 1)

                def finish(half, slot, nodes, layer=layer, to_table=to_table):
                    q = position(layer, half, slot)
                    part = LAST if nodes == LAST else P
                    count = 1 if nodes == LAST else SUB
                    if layer == 1:
                        act.wait_ge(y_ready, q + 3)
                        nc.scalar.activation(rows(scaled, nodes), rows(new[:, slot], nodes),
                                             ACT.Sigmoid).then_inc(sigmoid_done, 1)
                    else:
                        act.wait_ge(ln_step, ln_steps(layer, half, slot) + 2)
                        free(act, rows_ready, q)
                        nc.scalar.activation(std[0:part, 0:count], moments[0:part, 0:count, 1],
                                             ACT.Sqrt, bias=eps_col[0:part]
                                             ).then_inc(std_ready, 1)
                    if layer < 2:
                        act.wait_ge(rows_ready, q + 1)
                        nc.scalar.activation(table_rows(to_table, half, slot, nodes, 0),
                                             rows(new[:, slot], nodes), ACT.Copy
                                             ).then_inc(hi_ready, 1)
                        act.wait_ge(rest_ready, q + 1)
                        nc.scalar.activation(table_rows(to_table, half, slot, nodes, 1),
                                             rows(scaled, nodes), ACT.Copy, scale=SPLIT
                                             ).then_inc(lo_ready, 1)

                lead_and_post(act, layer, lead, post, turn, finish)
            general_scalar(act)

        @block.tensor
        def _(pe):
            def count(group, slot):
                pe.wait_ge(v_hot, group + 1)
                pe.wait_ge(p_hot, group + 2)
                pe.wait_ge(copied, group + 1)
                cut = HALF * WINDOW
                low, high = 2 * slot, 2 * slot + 1
                for t in range(GROUP):
                    first = t == 0
                    nc.tensor.matmul(ps[:, low, 0:cut], LOW[:, slot, t], M[:, slot, t, 0:cut],
                                     start=first, stop=not first, skip_group_check=True)
                    nc.tensor.matmul(ps[:, high, 0:COMBINED - cut], LOW[:, slot, t],
                                     M[:, slot, t, cut:COMBINED],
                                     start=first, stop=not first, skip_group_check=True)
                    last = nc.tensor.matmul(ps[:, high, COMBINED - cut:cut],
                                            TYPE[:, slot, t], WIN[:, slot, t],
                                            start=False, stop=not first, skip_group_check=True)
                last.then_inc(counted, 1)

            def multiply(b, chunk_at):
                for part, bank in ((0, EARLY_HI), (1, EARLY_LO)):
                    last = nc.tensor.matmul(ps[:, bank, :], table0[:, b, part, :],
                                            A[:, b, chunk_at], start=b == 0,
                                            stop=b == ROWS - 1, skip_group_check=True)
                return last

            def early_start(k):
                pe.wait_ge(early_summed, k + 1)
                multiply(0, columns_of(k))

            def early_end(k):
                multiply(ROWS - 1, columns_of(k)).then_inc(early_done, 1)

            def columns_of(k):
                return bass.ds(k * CHUNK, CHUNK) if not isinstance(k, int) else slice(
                    k * CHUNK, (k + 1) * CHUNK)

            def step(first, count_of_groups, early_block=None):
                for j in range(count_of_groups):
                    count(first + j, j % DEPTH)
                    if early_block:
                        early_block(j)

            pe.wait_ge(x_lo, 2)
            build(pe, step, early_start, lambda k, b: multiply(b, columns_of(k)), early_end)

            pe.wait_ge(copied, GROUPS + 2)
            pe.wait_ge(early_summed, EARLY + 1)
            pe.wait_ge(constants, 8)
            pe.wait_ge(weights_in, 16 * 14)

            def aggregate(layer, half, slot, nodes):
                table = (table0, table1, table0)[layer]
                blocks = ROWS if layer == 0 else BLOCKS
                at = nodes_at(half, slot, nodes)
                for b in range(blocks):
                    if layer and isinstance(half, int) and half == slot == 0 and b % SUB == 0:
                        pe.wait_ge(lo_ready, (layer - 1) * CHUNKS + b // SUB + 1)
                    for part in range(2):
                        last = nc.tensor.matmul(ps[:, 2 * slot + part, 0:nodes],
                                                table[:, b, part, :], A[:, b, at],
                                                start=b == 0, stop=b == blocks - 1)
                last.then_inc(agg_done, 1)

            for b in range(BLOCKS):
                size = min(P, N - b * P)
                last = nc.tensor.matmul(ps[0:size, DEG, b:b + 1],
                                        A[:, BLOCKS, b * P:b * P + size], ones_h[:, 0:1],
                                        start=True, stop=True)
            last.then_inc(deg_done, 1)
            for chunk in range(EARLY, CHUNKS):
                aggregate(0, chunk // 2, chunk % 2, CHUNK if chunk < CHUNKS - 1 else LAST)
            pe.wait_ge(weights_ready, 3)
            pe.wait_ge(rdeg_ready, 1)
            for layer in range(3):
                def lead(half, slot, nodes, layer=layer):
                    q = position(layer, half, slot)
                    if layer:
                        pe.wait_ge(summed, aggregated(layer, half, slot) - 1)
                        aggregate(layer, half, slot, nodes)

                def turn(half, slot, nodes, layer=layer):
                    pe.wait_ge(own_loaded[slot], before(layer, half, slot) * 16 + 16)
                    free(pe, own_T_ready, position(layer, half, slot))
                    for t in range(1 if nodes == LAST else SUB):
                        size = min(P, nodes)
                        last = nc.tensor.transpose(ps[:, TURN, t * P:t * P + size],
                                                   own[0:size, t, :],
                                                   ident[0:size, 0:size])
                    last.then_inc(turned, 1)

                def post(half, slot, nodes, layer=layer):
                    q = position(layer, half, slot)
                    tiles = [(min(P, nodes), t, slice(t * P, t * P + min(P, nodes)))
                             for t in range(1 if nodes == LAST else SUB)]
                    if layer or 2 * half + slot >= EARLY:
                        pe.wait_ge(summed, aggregated(layer, half, slot) + 1)
                    else:
                        pe.wait_ge(sum_loaded[slot], 16 * half + 16)
                    free(pe, messages_scaled, q)
                    for size, t, at in tiles:
                        last = nc.tensor.matmul(ps[0:size, MESSAGES, t * D:(t + 1) * D],
                                                sum_T[:, slot, at], weights[:, 2 * layer, :],
                                                start=True, stop=True)
                    last.then_inc(messages_done, 1)
                    pe.wait_ge(own_T_ready, q + 1)
                    pe.wait_ge(y_ready, q + 1)
                    for size, t, at in tiles:
                        to = ps[0:size, DENSE + slot, t * D:(t + 1) * D]
                        nc.tensor.matmul(to, own_T[:, at], weights[:, (6, 3, 5)[layer], :],
                                         start=True, stop=False)
                        last = nc.tensor.matmul(to, bias_scale[:, 0:size],
                                                bias_h[:, (2, 0, 1)[layer], :],
                                                start=False, stop=True)
                    last.then_inc(dense_done, 1)

                if layer == 2:
                    pe.wait_ge(any_ready, 1)
                    nc.tensor.matmul(ps[0:1, DEG, 0:1], any_over, ones_col,
                                     start=True, stop=True).then_inc(over_counted, 1)
                lead_and_post(pe, layer, lead, post, turn)
            general_tensor(pe)

        @block.vector
        def _(dve):
            nc.vector.memset(stage_x[:, BLOCKS - 1:ROWS, :], 0.0).then_inc(pads_zero, 1)
            nc.vector.memset(zeros, 0.0).then_inc(zeros_ready, 1)
            nc.vector.memset(carry[:], 0.0).then_inc(carried, 1)
            nc.vector.memset(edge_f[:, TILES:PADDED, :], -1.0)
            nc.vector.memset(delta_i[:, GROUPS - 1:GROUPS], 0)
            nc.vector.memset(peaks, 0.0)
            nc.vector.memset(limits[:, 0:1], (WINDOW - 1) / 2)
            nc.vector.memset(limits[:, 1:2], 0.0)
            nc.vector.memset(limits[:, 2:3], MOST_VALUE)
            nc.vector.memset(limits[:, 3:4], MOST_EDGES / 2 - 1)
            nc.vector.memset(limits[:, 4:PEAKS], MOST_VALUE)
            nc.vector.memset(floors[:, 0:LEAD - DEPTH], 0.0)
            for k in range(EARLY):
                end = LEAD - DEPTH + (k + 1) * PERIOD if k < EARLY - 1 else GROUPS
                nc.vector.memset(floors[:, LEAD - DEPTH + k * PERIOD:end],
                                 float(CHUNK * (k + 1)))
            nc.vector.engine_nop().then_inc(edge_step, 1)
            dve.wait_ge(edge_step, 1)
            nc.vector.memset(floors[:, GROUPS - 1:GROUPS], float(N - WINDOW)
                             ).then_inc(edge_step, 1)
            zero_first(nc.vector.memset, 17, ROWS)
            nc.vector.engine_nop().then_inc(counted, 2)
            nc.vector.engine_nop().then_inc(joined, 1)
            nc.vector.engine_nop().then_inc(early_summed, 1)
            nc.vector.engine_nop().then_inc(early_free, 1)
            nc.vector.engine_nop().then_inc(y_ready, 2)

            dve.wait_ge(edges_in, 64)
            nc.vector.memset(first_i[:, 0:1], 0)
            nc.vector.tensor_scalar(low_i, src_i, P - 1, None, ALU.bitwise_and)
            nc.vector.tensor_scalar(block_i, src_i, P.bit_length() - 1, None,
                                    ALU.arith_shift_right)
            nc.vector.tensor_scalar(type_f, type_i, 0, RELATIONS - 1, ALU.max, ALU.min
                                    ).then_inc(edge_step, 1)
            dve.wait_ge(edge_step, 3)
            nc.vector.tensor_tensor(base_i, floors, first_i, ALU.max).then_inc(edge_step, 1)
            nc.vector.tensor_copy(low_f[:, 0:TILES], low_i)
            dve.wait_ge(edge_step, 4)
            nc.vector.tensor_scalar(base_i[:, 0:LEAD], base_i[:, 0:LEAD], QUARTER - WINDOW, None,
                                    ALU.min).then_inc(edge_step, 1)
            dve.wait_ge(edge_step, 5)
            nc.vector.tensor_tensor(offset_f.rearrange("p (g t) -> p g t", t=GROUP),
                                    dst_i.rearrange("p (g t) -> p g t", t=GROUP),
                                    base_i.unsqueeze(2).to_broadcast([P, GROUPS, GROUP]),
                                    ALU.subtract)
            nc.vector.tensor_tensor(delta_i[:, 0:GROUPS - 1], base_i[:, 1:GROUPS],
                                    base_i[:, 0:GROUPS - 1], ALU.subtract
                                    ).then_inc(edge_step, 1)
            dve.wait_ge(edge_step, 6)
            nc.vector.scalar_tensor_tensor(combined_f, block_i, float(WINDOW), offset_f,
                                           ALU.mult, ALU.add)
            nc.vector.tensor_scalar(delta_i, delta_i, 0, WINDOW - 1, ALU.max, ALU.min
                                    ).then_inc(edge_step, 1)
            dve.wait_ge(edge_step, 7)
            nc.vector.engine_nop().then_inc(scalars_ready, 1)
            for k in range(2):
                half = slice(k * HALF, (k + 1) * HALF)
                dve.wait_ge(x_hi, k + 1)
                nc.vector.tensor_tensor(stage_x[:, half], stage_x[:, half],
                                        table0[:, half, 0, :], ALU.subtract
                                        ).then_inc(x_rest, 1)
            dve.wait_ge(constants, 8)

            def one_hots(group, slot):
                tile = group * GROUP
                nc.vector.tensor_tensor(
                    WIN[:, slot],
                    iota_p[:, 0:WINDOW].unsqueeze(1).to_broadcast([P, GROUP, WINDOW]),
                    edge_f[:, columns(tile), 2:3].to_broadcast([P, GROUP, WINDOW]),
                    ALU.is_equal)
                if slot == 1:
                    nc.vector.tensor_scalar(LOW[:, slot, 1], iota_p,
                                            edge_f[:, column(tile + 1), 1], None, ALU.is_equal)
                for t in range(GROUP):
                    nc.vector.tensor_scalar(TYPE[:, slot, t], iota_p,
                                            edge_f[:, column(tile + t), 3], None, ALU.is_equal)
                    last = nc.vector.tensor_scalar(M[:, slot, t], iota_c,
                                                   edge_f[:, column(tile + t), 0],
                                                   None, ALU.is_equal)
                last.then_inc(v_hot, 1)

            def join(group, slot):
                dve.wait_ge(counted, group + 3)
                dve.wait_ge(carried, group + 1)
                first = counts_of(slot)[:, :, :, 0:1]
                nc.vector.tensor_tensor(first, first, carry[:, slot], ALU.add
                                        ).then_inc(joined, 1)

            def step(first, count, _=None):
                for j in range(count):
                    one_hots(first + (j + 1), (j + 1) % DEPTH)
                    join(first + j, j % DEPTH)

            def early_end(k):
                dve.wait_ge(early_scaled, k + 1)
                nc.vector.tensor_tensor(early_sum, ps[:, EARLY_HI], early_sum, ALU.add
                                        ).then_inc(early_summed, 1)

            one_hots(0, 0)
            build(dve, step, early_end=early_end)

            dve.wait_ge(counted, GROUPS + 2)
            dve.wait_ge(v_hot, GROUPS + 1)
            middle = -(WINDOW - 1) / 2
            rest = E - FULL_TILES * P
            nc.vector.memset(off_middle[:, FULL_TILES:TILES], 0.0)
            nc.vector.memset(late[:, TILES - GROUP:TILES], 0.0).then_inc(check_step, 1)
            dve.wait_ge(check_step, 1)
            nc.vector.tensor_scalar(off_middle[:, 0:FULL_TILES], offset_f[:, 0:FULL_TILES],
                                    middle, None, ALU.add)
            nc.vector.tensor_scalar(off_middle[0:rest, FULL_TILES:TILES],
                                    offset_f[0:rest, FULL_TILES:TILES], middle, None, ALU.add)
            nc.vector.tensor_tensor(off_middle[:, TILES:TILES + GROUPS - 1],
                                    base_i[:, 1:GROUPS], base_i[:, 0:GROUPS - 1],
                                    ALU.subtract).then_inc(check_step, 1)
            dve.wait_ge(check_step, 2)
            steps = off_middle[:, TILES:TILES + GROUPS - 1]
            nc.vector.tensor_tensor(
                late[:, 0:TILES - GROUP].rearrange("p (g t) -> p g t", t=GROUP),
                offset_f[:, 0:TILES - GROUP].rearrange("p (g t) -> p g t", t=GROUP),
                steps.unsqueeze(2).to_broadcast([P, GROUPS - 1, GROUP]), ALU.subtract
            ).then_inc(check_step, 1)
            dve.wait_ge(check_step, 3)
            nc.vector.tensor_scalar(steps, steps, middle, None, ALU.add)
            nc.vector.tensor_reduce(peaks[:, 1:2], late, AX.X, ALU.max)
            nc.vector.tensor_reduce(peaks[:, 2:3], table0[:, :, 0, :], AX.XY, ALU.max,
                                    apply_absolute_value=True).then_inc(check_step, 1)
            dve.wait_ge(check_step, 4)
            nc.vector.tensor_reduce(peaks[:, 0:1], off_middle[:, 0:TILES + GROUPS - 1], AX.X,
                                    ALU.max, apply_absolute_value=True
                                    ).then_inc(edges_checked, 1)

            dve.wait_ge(edges_checked, 1)
            dve.wait_ge(copied, GROUPS + 2)
            dve.wait_ge(early_stored, 16 * EARLY)
            nc.vector.memset(table1[:, BLOCKS - 1], 0.0)
            nc.vector.memset(bias_scale, 0.0).then_inc(bias_step, 1)
            dve.wait_ge(bias_step, 1)
            nc.vector.memset(bias_scale[0:1], 1.0)
            nc.vector.memset(bias_scale[32:33], 1.0 / SPLIT).then_inc(weights_ready, 1)
            dve.wait_ge(weights_in, 16 * 14)
            nc.vector.tensor_tensor(bias[:, 3, :], bias[:, 3, :], bias[:, 0, :], ALU.add
                                    ).then_inc(bias_step, 1)
            nc.vector.tensor_tensor(weights[:, 6, :], weights[:, 1, :], ident[:], ALU.add
                                    ).then_inc(weights_ready, 1)
            dve.wait_ge(bias_step, 2)
            nc.vector.tensor_copy(bias_h, bias[:, 1:4, :]).then_inc(bias_step, 1)
            rest = scaled[32:33, 0:3, :]
            dve.wait_ge(bias_step, 3)
            nc.vector.tensor_tensor(rest, bias[32:33, 1:4, :], bias_h[32:33], ALU.subtract
                                    ).then_inc(bias_step, 1)
            dve.wait_ge(bias_step, 4)
            nc.vector.tensor_scalar(bias_h[32:33], rest, SPLIT, None, ALU.mult
                                    ).then_inc(weights_ready, 1)

            nc.vector.memset(degree, MOST_EDGES / 2).then_inc(deg_step, 1)
            dve.wait_ge(deg_step, 1)
            dve.wait_ge(deg_done, 1)
            nc.vector.tensor_copy(degree[:, 0:BLOCKS - 1], ps[:, DEG, 0:BLOCKS - 1])
            nc.vector.tensor_copy(degree[0:LAST, BLOCKS - 1:BLOCKS],
                                  ps[0:LAST, DEG, BLOCKS - 1:BLOCKS]).then_inc(deg_step, 1)
            dve.wait_ge(deg_step, 2)
            nc.vector.tensor_scalar(rdeg, degree, 1.0, None, ALU.max).then_inc(deg_step, 1)
            dve.wait_ge(deg_step, 3)
            nc.vector.reciprocal(rdeg, rdeg).then_inc(rdeg_ready, 1)
            nc.vector.tensor_scalar(degree, degree, -MOST_EDGES / 2, None, ALU.add
                                    ).then_inc(deg_step, 1)
            dve.wait_ge(deg_step, 4)
            nc.vector.tensor_reduce(peaks[:, 3:4], degree, AX.X, ALU.max,
                                    apply_absolute_value=True).then_inc(deg_step, 1)

            def peak(half, slot):
                return column(4 + half * 2 + slot)

            for layer in range(3):
                def lead(half, slot, nodes, layer=layer):
                    if layer or 2 * half + slot >= EARLY:
                        dve.wait_ge(lo_scaled, aggregated(layer, half, slot) + 1)
                        nc.vector.tensor_tensor(sum_T[:, slot, 0:nodes],
                                                ps[:, 2 * slot, 0:nodes],
                                                sum_T[:, slot, 0:nodes], ALU.add
                                                ).then_inc(summed, 1)

                def post(half, slot, nodes, layer=layer):
                    q = position(layer, half, slot)
                    size = min(P, nodes)
                    count = 1 if nodes == LAST else SUB
                    mine = new[:, slot]
                    free(dve, rows_stored[slot], before(layer, half, slot) * 16)
                    dve.sem_inc(waited, 1)
                    products = dense_rows(DENSE + slot, nodes)
                    dve.wait_ge(messages_scaled, q + 1)
                    dve.wait_ge(dense_done, q + 1)
                    if layer == 1:
                        nc.vector.tensor_tensor(rows(mine, nodes), products,
                                                rows(scaled, nodes), ALU.add
                                                ).then_inc(y_ready, 1)
                        dve.wait_ge(sigmoid_done, half * 2 + (slot + 1))
                        nc.vector.tensor_tensor(rows(mine, nodes), rows(mine, nodes),
                                                rows(scaled, nodes), ALU.mult
                                                ).then_inc(rows_ready, 1)
                    else:
                        if layer == 2:
                            nc.vector.tensor_tensor(rows(mine, nodes), products,
                                                    rows(scaled, nodes), ALU.add
                                                    ).then_inc(z_ready, 1)
                            dve.wait_ge(z_ready, half * 2 + (slot + 1))
                            dve.wait_ge(residual_loaded, (half * 2 + (slot + 1)) * 16)
                            nc.vector.tensor_tensor(rows(mine, nodes), rows(mine, nodes),
                                                    rows(residual, nodes), ALU.add
                                                    ).then_inc(y_ready, 1)
                        else:
                            nc.vector.tensor_tensor(rows(mine, nodes), products,
                                                    rows(scaled, nodes), ALU.add
                                                    ).then_inc(y_ready, 1)
                        dve.wait_ge(y_ready, q + 3)
                        step = ln_steps(layer, half, slot)
                        for t in range(count):
                            last = nc.vector.bn_stats(stats[0:size, t], mine[0:size, t])
                        last.then_inc(ln_step, 1)
                        dve.wait_ge(ln_step, step + 1)
                        free(dve, rows_ready, q)
                        dve.sem_inc(waited, 1)
                        for t in range(count):
                            last = nc.vector.bn_aggr(moments[0:size, t], stats[0:size, t])
                        last.then_inc(ln_step, 1)
                        dve.wait_ge(std_ready, ln_chunks(layer, half, slot) + 1)
                        nc.vector.reciprocal(std[0:size, 0:count], std[0:size, 0:count]
                                             ).then_inc(ln_step, 1)
                        dve.wait_ge(ln_step, step + 3)
                        for t in range(count):
                            last = nc.vector.tensor_scalar(
                                mine[0:size, t], mine[0:size, t], moments[0:size, t, 0:1],
                                std[0:size, t:t + 1], ALU.subtract, ALU.mult)
                        last.then_inc(rows_ready, 1)
                    if layer < 2:
                        dve.wait_ge(rows_ready, q + 1)
                        if layer == 1:
                            values = mine[0:size, 0:count]
                            nc.vector.tensor_reduce(peaks[0:size, peak(half, slot)], values,
                                                    AX.XY, ALU.max, apply_absolute_value=True)
                        dve.wait_ge(hi_ready, q + 1)
                        nc.vector.tensor_tensor(
                            rows(scaled, nodes), rows(mine, nodes),
                            table_rows((table1, table0)[layer], half, slot, nodes, 0),
                            ALU.subtract).then_inc(rest_ready, 1)

                if layer == 2:
                    dve.wait_ge(rest_ready, 2 * CHUNKS)
                    dve.wait_ge(deg_step, 5)
                    nc.vector.tensor_tensor(over, peaks, limits, ALU.is_gt).then_inc(over_step, 1)
                    dve.wait_ge(over_step, 1)
                    nc.vector.tensor_reduce(any_over, over, AX.X, ALU.max).then_inc(any_ready, 1)
                    dve.wait_ge(over_counted, 1)
                    nc.vector.tensor_copy(flag[0:1, :], ps[0:1, DEG, 0:1]).then_inc(flag_ready, 1)
                lead_and_post(dve, layer, lead, post)
            general_vector(dve)


def kernel(**inputs):
    import concourse.bacc as bacc
    from concourse.bass_utils import run_bass_kernel_spmd

    arrays = {}

    def lay(name, array):
        arrays[name] = np.ascontiguousarray(array)

    def edges(a, pad):
        a = np.asarray(a)
        padded = np.full(TILES * P, pad, a.dtype)
        padded[0:E] = a
        return padded.reshape(TILES, P).T

    dst = edges(inputs["dst"], NO_NODE)
    lay("x", inputs["x"])
    lay("src_t", edges(inputs["src"], 0))
    lay("dst_t", dst)
    lay("type_t", edges(inputs["edge_type_64"], 0))
    lay("first_dst", dst[0, ::GROUP])
    lay("rel_emb", inputs["L0_gnn_rel_emb"])
    for name, given in (("w_msg", "L0_gnn_W_msg"), ("w_self", "L0_gnn_W_self"),
                        ("w1_l", "L1_gnn_W1_l"), ("w1_r", "L1_gnn_W1_r"),
                        ("w2_l", "L1_gnn_W2_l"), ("w2_r", "L1_gnn_W2_r")):
        lay(name, np.asarray(inputs[given]).T)
    for name, given in (("b_self", "L0_gnn_b_self"), ("b_msg", "L0_gnn_b_msg"),
                        ("b1", "L1_gnn_b1"), ("b2", "L1_gnn_b2")):
        lay(name, np.asarray(inputs[given]).reshape(1, D))

    nc = bacc.Bacc("TRN2", target_bir_lowering=False, num_devices=1)
    args = {name: nc.dram_tensor(name, a.shape, mybir.dt.from_np(a.dtype),
                                 kind="ExternalInput").ap() for name, a in arrays.items()}
    for name, shape in (("x1_dram", (N, D)), ("h_dram", (N, D)), 
                        ("sum_dram", (P, EARLY * CHUNK))):
        args[name] = nc.dram_tensor(name, shape, F32, kind="Internal").ap()
    args["out"] = nc.dram_tensor("out", (N, D), F32, kind="ExternalOutput").ap()
    gnn_program(nc, **args)
    return run_bass_kernel_spmd(nc, [arrays], core_ids=[0]).results[0]["out"]
```
